# Optimizing a Trainium2 kernel written in Bass

```python
import numpy as np
import jax
import jax.numpy as jnp

def _softmax(x, axis=-1):
    return jax.nn.softmax(x, axis=axis)

def _gelu(x):
    return jax.nn.gelu(x, approximate=True)

def _silu(x):
    return jax.nn.silu(x)

def _sigmoid(x):
    return jax.nn.sigmoid(x)

def _layernorm(x, axis=-1, eps=1e-05):
    m = jnp.mean(x, axis=axis, keepdims=True)
    v = jnp.var(x, axis=axis, keepdims=True)
    return (x - m) / jnp.sqrt(v + eps)

def _scatter_add(tgt, idx, src, axis=0):
    return tgt.at[idx].add(src)

def _segment_sum(src, seg, n):
    return jax.ops.segment_sum(src, seg, n)
kernel_name = 'mk_cond_resid_d4_seqx_r8_019a22'

def setup_inputs(seed: int=0):
    np.random.seed(seed)
    _w = jnp.asarray

    def _rec_inputs():
        import jax
        import jax.numpy as jnp
        _rk = jax.random.key(seed)
        x = -7.109e-05 + 0.9999 * jax.random.normal(jax.random.fold_in(_rk, 1), (32, 32, 512), jnp.float32)
        _lenS = 32 - jax.random.randint(jax.random.fold_in(_rk, 7), (32,), 0, max(1, 32 // 4) + 1, jnp.int32)
        _lenS2 = 32 - jax.random.randint(jax.random.fold_in(_rk, 8), (32,), 0, max(1, 32 // 4) + 1, jnp.int32)
        itok_B_0_15 = jax.random.randint(jax.random.fold_in(_rk, 11), (32,), 0, 16, jnp.int32)
        itok_Bx16_0_63 = jax.random.randint(jax.random.fold_in(_rk, 12), (32, 16), 0, 64, jnp.int32)
        itok_B_207_1644 = jax.random.randint(jax.random.fold_in(_rk, 13), (32,), 207, 1645, jnp.int32)
        itok_B_0_30 = jax.random.randint(jax.random.fold_in(_rk, 14), (32,), 0, 31, jnp.int32)
        itok_B_0_7 = jax.random.randint(jax.random.fold_in(_rk, 15), (32,), 0, 8, jnp.int32)
        return (x, itok_B_0_15, itok_Bx16_0_63, itok_B_207_1644, itok_B_0_30, itok_B_0_7)
    x, itok_B_0_15, itok_Bx16_0_63, itok_B_207_1644, itok_B_0_30, itok_B_0_7 = _rec_inputs()

    def _L0_cond_setup():
        import jax, jax.numpy as jnp
        import numpy as np
        MAX_LORAS = 16
        IN, OUT = (512, 512)
        B, S = (8, 256)
        key = jax.random.key(seed)
        k1, k2, k3 = jax.random.split(key, 3)
        x = jax.random.normal(k1, (B, S, IN), dtype=jnp.float32)
        adapter_ids = jax.random.randint(k2, (B,), 0, MAX_LORAS)
        weight = jax.random.normal(k3, (MAX_LORAS, OUT, IN), dtype=jnp.float32) * 0.02
        return {'x': x, 'adapter_ids': adapter_ids, 'weight': weight}
    _L0_cond_all = _L0_cond_setup()
    _L0_cond_in = {k: v for k, v in _L0_cond_all.items() if k in ('weight',)}
    del _L0_cond_all

    def _L1_cond_setup():
        import jax, jax.numpy as jnp
        import numpy as np
        B, S, HID = (4, 128, 512)
        D, HQ, HK = (128, 32, 8)
        PAGES, PSIZE, NPP = (64, 32, 16)
        THETA = 10000.0
        EPS = 1e-06
        SCALE = 1.0 / float(np.sqrt(D))

        def _rmsnorm(t, w):
            var = jnp.mean(t * t, axis=-1, keepdims=True)
            return t * jax.lax.rsqrt(var + EPS) * w

        def _rope(t, pos):
            inv_freq = 1.0 / THETA ** (jnp.arange(0, D, 2, dtype=jnp.float32) / D)
            freqs = pos[..., None].astype(jnp.float32) * inv_freq
            cos = jnp.cos(freqs)[:, :, None, :]
            sin = jnp.sin(freqs)[:, :, None, :]
            t1, t2 = (t[..., :D // 2], t[..., D // 2:])
            return jnp.concatenate([t1 * cos - t2 * sin, t2 * cos + t1 * sin], axis=-1)
        key = jax.random.key(seed)
        ks = jax.random.split(key, 10)
        x = jax.random.normal(ks[0], (B, S, HID), jnp.float32)
        Wq = jax.random.normal(ks[1], (HQ * D, HID), jnp.float32) * 0.02
        Wk = jax.random.normal(ks[2], (HK * D, HID), jnp.float32) * 0.02
        Wv = jax.random.normal(ks[3], (HK * D, HID), jnp.float32) * 0.02
        Wo = jax.random.normal(ks[4], (HID, HQ * D), jnp.float32) * 0.02
        q_norm_w = jax.random.uniform(ks[5], (D,), jnp.float32)
        k_norm_w = jax.random.uniform(ks[6], (D,), jnp.float32)
        k_cache = jax.random.normal(ks[7], (PAGES, PSIZE, HK, D), jnp.float32)
        v_cache = jax.random.normal(ks[8], (PAGES, PSIZE, HK, D), jnp.float32)
        block_table = jnp.arange(B * NPP, dtype=jnp.int32).reshape(B, NPP)
        cache_seqlens = jax.random.randint(ks[9], (B,), 0, 475).astype(jnp.int32)
        return dict(x=x, Wq=Wq, Wk=Wk, Wv=Wv, Wo=Wo, q_norm_w=q_norm_w, k_norm_w=k_norm_w, k_cache=k_cache, v_cache=v_cache, block_table=block_table, cache_seqlens=cache_seqlens)
    _L1_cond_all = _L1_cond_setup()
    _L1_cond_in = {k: v for k, v in _L1_cond_all.items() if k in ('Wq', 'Wk', 'Wv', 'Wo', 'q_norm_w', 'k_norm_w', 'k_cache', 'v_cache')}
    del _L1_cond_all

    def _L2_cond_setup():
        import jax, jax.numpy as jnp
        import numpy as np
        B, C, D, T, S = (64, 32, 32, 512, 32)
        key = jax.random.key(seed)
        k1, k2, k3 = jax.random.split(key, 3)
        x = jax.random.normal(k1, (B, C, T), dtype=jnp.float32)
        subjects = jax.random.randint(k2, (B,), 0, S, dtype=jnp.int64)
        weights = jax.random.normal(k3, (S, C, D), dtype=jnp.float32) * (1.0 / np.sqrt(C))
        return {'x': x, 'subjects': subjects, 'weights': weights}
    _L2_cond_all = _L2_cond_setup()
    _L2_cond_in = {k: v for k, v in _L2_cond_all.items() if k in ('weights',)}
    del _L2_cond_all

    def _L3_cond_setup():
        import jax, jax.numpy as jnp
        import numpy as np
        TOP_K = 2
        LANG_BIAS = 5.0
        SCALING = 32.0 / 16.0
        LANGUAGE_PAD_ID = -1
        key = jax.random.key(seed)
        ks = jax.random.split(key, 6)
        B, T, D, O, E, R = (4, 256, 512, 512, 8, 16)
        x = jax.random.normal(ks[0], (B, T, D), dtype=jnp.float32)
        language_ids = jax.random.randint(ks[1], (B,), 0, E).astype(jnp.int64)
        W = jax.random.normal(ks[2], (O, D), dtype=jnp.float32) * (1.0 / np.sqrt(D))
        Wr = jax.random.normal(ks[3], (E, D), dtype=jnp.float32) * (1.0 / np.sqrt(D))
        A = jax.random.normal(ks[4], (E, R, D), dtype=jnp.float32) * (1.0 / np.sqrt(D))
        Bm = jax.random.normal(ks[5], (O, R), dtype=jnp.float32) * 0.0
        Bm = jnp.broadcast_to(Bm, (E, O, R)) + jax.random.normal(ks[5], (E, O, R), dtype=jnp.float32) * 0.02
        return {'x': x, 'language_ids': language_ids, 'W': W, 'Wr': Wr, 'A': A, 'B': Bm}
    _L3_cond_all = _L3_cond_setup()
    _L3_cond_in = {k: v for k, v in _L3_cond_all.items() if k in ('W', 'Wr', 'A', 'B')}
    del _L3_cond_all
    return {'x': x, 'itok_B_0_15': itok_B_0_15, 'itok_Bx16_0_63': itok_Bx16_0_63, 'itok_B_207_1644': itok_B_207_1644, 'itok_B_0_30': itok_B_0_30, 'itok_B_0_7': itok_B_0_7, 'L0_cond_weight': _L0_cond_in['weight'], 'L1_cond_Wq': _L1_cond_in['Wq'], 'L1_cond_Wk': _L1_cond_in['Wk'], 'L1_cond_Wv': _L1_cond_in['Wv'], 'L1_cond_Wo': _L1_cond_in['Wo'], 'L1_cond_q_norm_w': _L1_cond_in['q_norm_w'], 'L1_cond_k_norm_w': _L1_cond_in['k_norm_w'], 'L1_cond_k_cache': _L1_cond_in['k_cache'], 'L1_cond_v_cache': _L1_cond_in['v_cache'], 'L2_cond_weights': _L2_cond_in['weights'], 'L3_cond_W': _L3_cond_in['W'], 'L3_cond_Wr': _L3_cond_in['Wr'], 'L3_cond_A': _L3_cond_in['A'], 'L3_cond_B': _L3_cond_in['B']}

def reference(x, itok_B_0_15, itok_Bx16_0_63, itok_B_207_1644, itok_B_0_30, itok_B_0_7, L0_cond_weight, L1_cond_Wq, L1_cond_Wk, L1_cond_Wv, L1_cond_Wo, L1_cond_q_norm_w, L1_cond_k_norm_w, L1_cond_k_cache, L1_cond_v_cache, L2_cond_weights, L3_cond_W, L3_cond_Wr, L3_cond_A, L3_cond_B):
    import jax
    import jax.numpy as jnp

    def _L0_cond_ref(x, adapter_ids, weight):
        import jax, jax.numpy as jnp
        import numpy as np
        MAX_LORAS = 16
        IN, OUT = (512, 512)
        B, S = (8, 256)
        w = weight[adapter_ids]
        return jnp.einsum('bsi,boi->bso', x, w)

    def _L1_cond_ref(x, Wq, Wk, Wv, Wo, q_norm_w, k_norm_w, k_cache, v_cache, block_table, cache_seqlens):
        import jax, jax.numpy as jnp
        import numpy as np
        B, S, HID = (4, 128, 512)
        D, HQ, HK = (128, 32, 8)
        PAGES, PSIZE, NPP = (64, 32, 16)
        THETA = 10000.0
        EPS = 1e-06
        SCALE = 1.0 / float(np.sqrt(D))

        def _rmsnorm(t, w):
            var = jnp.mean(t * t, axis=-1, keepdims=True)
            return t * jax.lax.rsqrt(var + EPS) * w

        def _rope(t, pos):
            inv_freq = 1.0 / THETA ** (jnp.arange(0, D, 2, dtype=jnp.float32) / D)
            freqs = pos[..., None].astype(jnp.float32) * inv_freq
            cos = jnp.cos(freqs)[:, :, None, :]
            sin = jnp.sin(freqs)[:, :, None, :]
            t1, t2 = (t[..., :D // 2], t[..., D // 2:])
            return jnp.concatenate([t1 * cos - t2 * sin, t2 * cos + t1 * sin], axis=-1)
        bsz, seqlen, _ = x.shape
        q = jnp.einsum('bsd,ed->bse', x, Wq).reshape(bsz, seqlen, HQ, D)
        k = jnp.einsum('bsd,ed->bse', x, Wk).reshape(bsz, seqlen, HK, D)
        v = jnp.einsum('bsd,ed->bse', x, Wv).reshape(bsz, seqlen, HK, D)
        q = _rmsnorm(q, q_norm_w)
        k = _rmsnorm(k, k_norm_w)
        pos = cache_seqlens[:, None] + jnp.arange(seqlen)[None, :]
        q = _rope(q, pos)
        k = _rope(k, pos)
        L = NPP * PSIZE
        kc = k_cache[block_table].reshape(bsz, L, HK, D)
        vc = v_cache[block_table].reshape(bsz, L, HK, D)
        k_all = jnp.concatenate([kc, k], axis=1)
        v_all = jnp.concatenate([vc, v], axis=1)
        valid_c = jnp.arange(L)[None, :] < cache_seqlens[:, None]
        valid = jnp.concatenate([valid_c, jnp.ones((bsz, seqlen), dtype=bool)], axis=1)
        rep = HQ // HK
        k_all = jnp.repeat(k_all, rep, axis=2)
        v_all = jnp.repeat(v_all, rep, axis=2)
        scores = jnp.einsum('bqhd,bkhd->bhqk', q, k_all) * SCALE
        scores = jnp.where(valid[:, None, None, :], scores, -1e+30)
        probs = jax.nn.softmax(scores, axis=-1)
        o = jnp.einsum('bhqk,bkhd->bqhd', probs, v_all)
        o = o.reshape(bsz, seqlen, HQ * D)
        return jnp.einsum('bse,de->bsd', o, Wo)

    def _L2_cond_ref(x, subjects, weights):
        import jax, jax.numpy as jnp
        import numpy as np
        B, C, D, T, S = (64, 32, 32, 512, 32)
        w = weights[subjects]
        return jnp.einsum('bct,bcd->bdt', x, w)

    def _L3_cond_ref(x, language_ids, W, Wr, A, B):
        import jax, jax.numpy as jnp
        import numpy as np
        TOP_K = 2
        LANG_BIAS = 5.0
        SCALING = 32.0 / 16.0
        LANGUAGE_PAD_ID = -1
        base = jnp.einsum('btd,od->bto', x, W)
        E = Wr.shape[0]
        logits = jnp.einsum('btd,ed->bte', x.astype(jnp.float32), Wr.astype(jnp.float32))
        expert_targets = language_ids
        valid = expert_targets >= 0
        tgt = jnp.where(valid, expert_targets, 0)
        bias = jax.nn.one_hot(tgt, E, dtype=logits.dtype) * LANG_BIAS
        bias = jnp.where(valid[:, None], bias, 0.0)
        logits = logits + bias[:, None, :]
        topw, topi = jax.lax.top_k(logits, TOP_K)
        weights = jax.nn.softmax(topw, axis=-1)
        gates = jnp.sum(jax.nn.one_hot(topi, E, dtype=weights.dtype) * weights[..., None], axis=-2)
        gates = gates.astype(x.dtype)
        h = jnp.einsum('btd,erd->bter', x, A)
        lora_out = jnp.einsum('bter,bte,eor->bto', h, gates, B)
        return base + SCALING * lora_out
    x = x + _L0_cond_ref(x, itok_B_0_15, L0_cond_weight)
    x = x + _L1_cond_ref(x, L1_cond_Wq, L1_cond_Wk, L1_cond_Wv, L1_cond_Wo, L1_cond_q_norm_w, L1_cond_k_norm_w, L1_cond_k_cache, L1_cond_v_cache, itok_Bx16_0_63, itok_B_207_1644)
    x = x + _L2_cond_ref(x, itok_B_0_30, L2_cond_weights)
    x = x + _L3_cond_ref(x, itok_B_0_7, L3_cond_W, L3_cond_Wr, L3_cond_A, L3_cond_B)
    return x

_drawn_inputs = setup_inputs


def setup_inputs(seed=0):
    import zlib

    import numpy as np

    out = dict(_drawn_inputs(seed))
    spreads = {}
    factors = {'L1_cond_Wk': 45.249,
     'L1_cond_Wv': 64.0,
     'L1_cond_q_norm_w': 2.736,
     'L1_cond_k_norm_w': 38.613,
     'L1_cond_k_cache': 8.0,
     'L1_cond_v_cache': 8.0}
    for name, (base, spread) in spreads.items():
        noise = np.random.default_rng([zlib.crc32(name.encode()), seed]).standard_normal(out[name].shape)
        drawn = base * np.exp(spread * noise) if base else spread * noise
        out[name] = jnp.asarray(drawn.astype(out[name].dtype))
    for name, factor in factors.items():
        out[name] = (out[name] * factor).astype(out[name].dtype)
    return out
```

```python
from contextlib import ExitStack

import numpy as np

import concourse.bass as bass
from concourse import mybir

F32 = mybir.dt.float32
F32R = mybir.dt.float32r
I32 = mybir.dt.int32
U32 = mybir.dt.uint32
ALU = mybir.AluOpType
ACT = mybir.ActivationFunctionType
AX_X = mybir.AxisListType.X
SP_ENGINE = mybir.EngineType.SP

P = 128
NB, SEQ, HID = 32, 32, 512
D, HQ, HK = 128, 32, 8
G = HQ // HK
PAGES, PSIZE, NPP = 64, 32, 16
L = NPP * PSIZE
KEYS = L + SEQ
NCH = L // P + 1
TB = P // SEQ
NT = NB // TB
KC = HID // P
QKV_BLOCKS = (HQ + 2 * HK) * D // HID
QK_BLOCKS = (HQ + HK) * D // HID
Q_BLOCKS = HQ * D // HID
QK_ROW = QK_BLOCKS * P
Q_COLS = Q_BLOCKS * P
PAD = P - SEQ
E, R = 8, 16
ER = E * R
SCALE = 1.0 / float(np.sqrt(D))
EPS = 1e-6
LANG_BIAS = 5.0
SCALING = 2.0
MASKED = -1e30

C_IDENT, C_FREQ, C_KEY, C_EXPERT, C_TOKEN = 0, P, P + D // 2, P + D // 2 + L, P + D // 2 + L + E
C_ALL = C_TOKEN + 1

TURN_A = 6.28125
TURN_B = float(np.round((2 * np.pi - TURN_A) * 2.0**21) / 2.0**21)
TURN_C = float(np.float32(2 * np.pi - TURN_A - TURN_B))
ROUND = 1.5 * 2.0**23
SIN_LIMIT = 3.1415925


def after_start(value):
    return not isinstance(value, int) or value > 0


def build(nc, x_tok, x_feat, adapter, pages, lens, subject, language, w0, wqkv, wo, kcache, vcache,
          q_w, k_w, w2, w3, a3, b3, consts, out):
    qk_dram = nc.dram_tensor("qk_scratch", (NB, D, QK_ROW), F32).ap()
    v_dram = nc.dram_tensor("v_scratch", (NB * SEQ, HK * D), F32).ap()
    x1_dram = nc.dram_tensor("x1_scratch", (NB * SEQ, HID), F32).ap()

    ctx = ExitStack()
    stage_a, stage_b = ExitStack(), ExitStack()
    with ctx:
        def sem(name):
            return ctx.enter_context(nc.semaphore(name))

        def keep(name, shape, dt=F32):
            return ctx.enter_context(nc.sbuf_tensor(name, shape, dt))

        const = keep("const", [P, C_ALL])
        ident = const[:, C_IDENT:C_IDENT + P]
        freq = const[:, C_FREQ:C_FREQ + D // 2]
        key_no = const[:, C_KEY:C_KEY + L]
        expert_no = const[:, C_EXPERT:C_EXPERT + E]
        token_no = const[:, C_TOKEN:C_TOKEN + 1]
        adapter_sb = keep("adapter_sb", [1, NB], I32)
        subject_sb = keep("subject_sb", [1, NB], I32)
        pages_all = keep("pages_all", [P, NB * NPP], I32)
        lens_f = keep("lens_f", [P, NB])
        v_rows = keep("v_rows", [P, NB * (NCH - 1)], U32)
        lang_bias = keep("lang_bias", [P, NT, E])

        def sa(name, shape, dt=F32):
            return stage_a.enter_context(nc.sbuf_tensor(name, shape, dt))

        def pa(name):
            return stage_a.enter_context(nc.psum_tensor(name, [P, HID], F32))

        w0_sb = sa("w0_sb", [P, 2, TB, KC, HID])
        x0t = sa("x0t", [P, 2, KC, P])
        x0 = sa("x0", [P, 2, HID])
        x1 = sa("x1", [P, 2, HID])
        x1t_hi = sa("x1t_hi", [P, KC, NT * P], F32R)
        x1t_lo = sa("x1t_lo", [P, KC, NT * P], F32R)
        w_raw = sa("w_raw", [P, 2, KC * HID])
        w_hi = sa("w_hi", [P, 2, KC * HID], F32R)
        w_lo = sa("w_lo", [P, 2, KC * HID], F32R)
        square = sa("square", [P, 2, HID])
        straight = sa("straight", [P, 4, HID])
        crossed = sa("crossed", [P, 2, HID])
        rotated = sa("rotated", [P, 2, HID])
        staged = sa("staged", [P, 2, HID])
        table = sa("table", [P, 4, NT, D])
        sumsq = sa("sumsq", [P, 4, G])
        meansq = sa("meansq", [P, 4, G])
        rstd = sa("rstd", [P, 4, G])
        minus_half = sa("minus_half", [P, G])
        qk_w = sa("qk_w", [P, 2, D])
        pos = sa("pos", [P, NT])
        lang_f = sa("lang_f", [P, NT])
        lens_all = sa("lens_all", [P, NB], I32)
        lang_all = sa("lang_all", [P, NB], I32)
        angle, turns = square[:, 0, :], square[:, 1, :]
        reduced = [crossed[:, i, :] for i in range(2)]
        l0_ps = [pa(f"l0_ps{i}") for i in range(2)]
        x1t_ps = pa("x1t_ps")
        proj_ps = [pa(f"proj_ps{i}") for i in range(2)]
        turn_ps = [pa(f"turn_ps{i}") for i in range(2)]
        stage_a.close()

        def sb(name, shape, dt=F32):
            return stage_b.enter_context(nc.sbuf_tensor(name, shape, dt))

        def pb(name):
            return stage_b.enter_context(nc.psum_tensor(name, [P, HID], F32))

        kt = sb("kt", [P, 2, NPP, HK * PSIZE])
        vt = sb("vt", [P, 2, NCH, HK * D])
        wo_sb = sb("wo_sb", [P, HQ, HID])
        qk_sb = sb("qk_sb", [P, 2, QK_ROW + PAD])
        probs = sb("probs", [P, 4, NCH * P])
        probs_t = sb("probs_t", [P, 2, NCH * P])
        mask = sb("mask", [P, KEYS])
        o_t = sb("o_t", [P, HQ, P])
        low = sb("low", [P, 4])
        total = sb("total", [P, 4])
        inverse = sb("inverse", [P, 4])
        v_now = sb("v_now", [P, NCH - 1], U32)
        w3_sb = sb("w3_sb", [P, KC, HID])
        a3_sb = sb("a3_sb", [P, KC, ER + E])
        b3_sb = sb("b3_sb", [P, HID])
        w2_sb = sb("w2_sb", [P, P])
        res1 = sb("res1", [P, HID])
        res2 = sb("res2", [P, HID])
        res3 = sb("res3", [P, HID])
        res3_t = sb("res3_t", [P, KC, P])
        hid = sb("hid", [P, ER + E])
        gated = hid[:, 0:ER]
        gated_t = sb("gated_t", [P, P])
        top = sb("top", [P, 8])
        top_at = sb("top_at", [P, 8], U32)
        gate = sb("gate", [P, 8])
        picks = sb("picks", [P, 3, E])
        s_ps = stage_b.enter_context(nc.psum_tensor("s_ps", [P, 2 * HID], F32))
        pt_ps = [pb(f"pt_ps{i}") for i in range(2)]
        pn_ps = [pb(f"pn_ps{i}") for i in range(2)]
        o_ps = pb("o_ps")
        acc = pb("acc")
        stage_b.close()

        s_const = sem("s_const")
        s_l0in = [sem(f"s_l0in{i}") for i in range(2)]
        s_x1out = sem("s_x1out")
        s_wraw = [sem(f"s_wraw{i}") for i in range(2)]
        s_stored = [sem(f"s_stored{i}") for i in range(2)]
        s_vstored = [sem(f"s_vstored{i}") for i in range(2)]
        s_index = sem("s_index")
        s_table = sem("s_table")
        s_angle = sem("s_angle")
        s_trig = sem("s_trig")
        s_l0 = sem("s_l0")
        s_x1 = sem("s_x1")
        s_x1turn = sem("s_x1turn")
        s_x1hi = sem("s_x1hi")
        s_x1lo = sem("s_x1lo")
        s_whi = sem("s_whi")
        s_wlo = sem("s_wlo")
        s_proj = sem("s_proj")
        s_square = sem("s_square")
        s_cross = sem("s_cross")
        s_sumsq = sem("s_sumsq")
        s_rstd = sem("s_rstd")
        s_rot = sem("s_rot")
        s_scaled = sem("s_scaled")
        s_turned = sem("s_turned")
        s_staged = sem("s_staged")

        s_blank = sem("s_blank")
        s_weights = sem("s_weights")
        s_k = [sem(f"s_k{i}") for i in range(2)]
        s_vnew = [sem(f"s_vnew{i}") for i in range(2)]
        s_v = [sem(f"s_v{i}") for i in range(2)]
        s_scores = sem("s_scores")
        s_low = sem("s_low")
        s_exp = sem("s_exp")
        s_inv = sem("s_inv")
        s_norm = sem("s_norm")
        s_pt = sem("s_pt")
        s_ptc = sem("s_ptc")
        s_pnc = sem("s_pnc")
        s_pv = sem("s_pv")
        s_o = sem("s_o")
        s_wo = sem("s_wo")
        s_tail_in = sem("s_tail_in")
        s_res2 = sem("s_res2")
        s_l2 = sem("s_l2")
        s_res3 = sem("s_res3")
        s_r3turn = sem("s_r3turn")
        s_r3t = sem("s_r3t")
        s_hid = sem("s_hid")
        s_gap = sem("s_gap")
        s_gexp = sem("s_gexp")
        s_gated = sem("s_gated")
        s_gturn = sem("s_gturn")
        s_gt = sem("s_gt")
        s_l3 = sem("s_l3")
        s_final = sem("s_final")
        s_out = sem("s_out")

        N_CONST = 8
        QK_UNITS, UNITS = QK_BLOCKS * NT, QKV_BLOCKS * NT
        BODY = 2 * NT
        PAIRS, TP = NB * HK, TB * HK
        K_DMAS = NPP + 1

        block = ctx.enter_context(nc.Block())

        @block.sync
        def _(sp):
            sp.dma_start(adapter_sb[:, :], adapter).then_inc(s_const, 16)
            sp.dma_start(subject_sb[:, :], subject).then_inc(s_const, 16)
            sp.dma_start(const[:, :], consts).then_inc(s_const, 16)
            sp.dma_start(lens_all[:, :], lens.partition_broadcast(P)).then_inc(s_const, 16)
            sp.dma_start(pages_all[:, :], pages.partition_broadcast(P)).then_inc(s_const, 16)
            sp.dma_start(lang_all[:, :], language.partition_broadcast(P)).then_inc(s_const, 16)
            sp.dma_start(qk_w[:, 0, :], q_w.partition_broadcast(P)).then_inc(s_const, 16)
            sp.dma_start(qk_w[:, 1, :], k_w.partition_broadcast(P)).then_inc(s_const, 16)
            sp.wait_ge(s_const, 16 * N_CONST)
            for t in range(NT):
                c = t % 2
                if t >= 2:
                    sp.wait_ge(s_l0, t - 1)
                    sp.wait_ge(s_x1, t - 1)
                sp.dma_start(x0t[:, c], x_feat[:, :, t * P:(t + 1) * P]).then_inc(s_l0in[c], 16)
                sp.dma_start(x0[:, c], x_tok[t * P:(t + 1) * P, :]).then_inc(s_l0in[c], 16)
                for b in range(TB):
                    a = sp.value_load(adapter_sb[0:1, TB * t + b:TB * t + b + 1], min_val=0,
                                      max_val=w0.shape[0] - 1)
                    sp.dma_start(w0_sb[:, c, b], w0[bass.ds(a, 1)].rearrange("o p c n -> (o p) c n"))\
                      .then_inc(s_l0in[c], 16)
                if t < 2:
                    sp.dma_start(w_raw[:, t], wqkv[t]).then_inc(s_wraw[t], 16)
                if t >= 1:
                    sp.wait_ge(s_x1, t)
                    sp.dma_start(x1_dram[(t - 1) * P:t * P, :], x1[:, (t - 1) % 2]).then_inc(s_x1out, 16)
            sp.wait_ge(s_x1, NT)
            sp.dma_start(x1_dram[(NT - 1) * P:NT * P, :], x1[:, (NT - 1) % 2]).then_inc(s_x1out, 16)

            def load_w(j, c):
                sp.wait_ge(s_wlo, j - 1)
                sp.dma_start(w_raw[:, c:c + 1], wqkv[bass.ds(j, 1)].rearrange("o p n -> p o n"))\
                  .then_inc(s_wraw[c], 16)

            def load_pages(b, c):
                _, page = nc.values_load_multi_w_load_instructions(
                    pages_all[0:1, bass.ds(b * NPP, NPP)], engines=[SP_ENGINE], min_val=0,
                    max_val=PAGES - 1)
                for j in range(NPP):
                    sp.dma_start(kt[:, c, j], kcache[bass.ds(page[j], 1)].rearrange("o d n -> (o d) n"))\
                      .then_inc(s_k[c], 16)

            load_w(2, 0)
            sp.wait_ge(s_l0, NT)
            load_pages(0, 0)
            load_pages(1, 1)

            def units(i):
                for n in range(BODY):
                    t, c = n % NT, n % 2
                    sp.wait_ge(s_staged, BODY * i + n + 1)
                    dst = qk_dram[TB * t:TB * t + TB, :, bass.ds((2 * i + n // NT) * P, P)]
                    sp.dma_start(dst.rearrange("b d n -> d b n"),
                                 staged[:, c].rearrange("d (b n) -> d b n", b=TB))\
                      .then_inc(s_stored[c], 16)
                    if n == 1:
                        load_w(2 * i + 3, 1)
                    if n == NT + 1 and not (isinstance(i, int) and 2 * i + 4 >= QKV_BLOCKS):
                        load_w(2 * i + 4, 0)

            with sp.Fori(0, QK_BLOCKS // 2 - 1) as i:
                units(i)
            units(QK_BLOCKS // 2 - 1)
            for u in range(QK_UNITS, UNITS):
                t, h, c = u % NT, u // NT - QK_BLOCKS, u % 2
                sp.wait_ge(s_square, u + 1)
                sp.dma_start(v_dram[t * P:(t + 1) * P, h * HID:(h + 1) * HID], square[:, c])\
                  .then_inc(s_vstored[c], 16)
            for c in range(2):
                sp.wait_ge(s_stored[c], 16 * QK_UNITS // 2)
                sp.wait_ge(s_vstored[c], 16 * (UNITS - QK_UNITS) // 2)
            sp.wait_ge(s_x1out, 16 * NT)

            def load_new(b, c):
                sp.dma_start(qk_sb[:, c:c + 1, 0:QK_ROW], qk_dram[bass.ds(b, 1)].rearrange("o d n -> d o n"))\
                  .then_inc(s_k[c], 16)
                sp.dma_start(vt[0:SEQ, c, NCH - 1], v_dram[bass.ds(b * SEQ, SEQ), :]).then_inc(s_vnew[c], 16)

            def load_tail(t):
                sp.dma_start(res1[:, :], x1_dram[bass.ds(t * P, P), :]).then_inc(s_tail_in, 16)
                _, subj = nc.values_load_multi_w_load_instructions(
                    subject_sb[0:1, bass.ds(t * TB, TB)], engines=[SP_ENGINE], min_val=0,
                    max_val=w2.shape[0] - 1)
                for b in range(TB):
                    q = slice(SEQ * b, SEQ * b + SEQ)
                    sp.dma_start(w2_sb[q, q], w2[bass.ds(subj[b], 1)].rearrange("o c d -> (o c) d"))\
                      .then_inc(s_tail_in, 16)

            sp.wait_ge(s_blank, 1)
            load_new(0, 0)
            load_new(1, 1)
            sp.dma_start(wo_sb[:, :, :], wo).then_inc(s_weights, 16)
            sp.dma_start(w3_sb[:, :, :], w3).then_inc(s_weights, 16)
            sp.dma_start(a3_sb[:, :, :], a3).then_inc(s_weights, 16)
            sp.dma_start(b3_sb[:, :], b3).then_inc(s_weights, 16)
            load_tail(0)

            def tile(t):
                for m in range(TB):
                    b, c = TB * t + m, m % 2
                    if isinstance(t, int) and b < 2:
                        continue
                    sp.wait_ge(s_scores, HK * (b - 1))
                    load_pages(b, c)
                    sp.wait_ge(s_pv, HK * (b - 1))
                    load_new(b, c)
                if isinstance(t, int) and t == 0:
                    return
                store_tile(t - 1)
                load_tail(t)

            def store_tile(t):
                sp.wait_ge(s_final, t + 1)
                sp.dma_start(out[bass.ds(t * P, P), :], res2[:, :]).then_inc(s_out, 16)

            tile(0)
            with sp.Fori(1, NT) as t:
                tile(t)
            store_tile(NT - 1)
            sp.wait_ge(s_out, 16 * NT)

        @block.gpsimd
        def _(pool):
            pool.memset(minus_half[:, :], -0.5)

            def gather(b, c):
                pool.tensor_copy(v_now[:, :], v_rows[:, bass.ds(b * (NCH - 1), NCH - 1)])
                pool.drain()
                for j in range(NCH - 1):
                    pool.indirect_dma_start(
                        vt[:, c, j], None, vcache,
                        bass.IndirectOffsetOnAxis(ap=v_now[:, j:j + 1], axis=0))\
                        .then_inc(s_v[c], 16)

            def units(i):
                for n in range(BODY):
                    u, c, r = BODY * i + n, n % 2, n % 4
                    pool.wait_ge(s_cross, u + 1)
                    pool.wait_ge(s_sumsq, u + 1)
                    pool.tensor_tensor(straight[:, r], straight[:, r], crossed[:, c], ALU.add)\
                        .then_inc(s_rot, 1)
                    pool.tensor_scalar(meansq[:, r], sumsq[:, r], 1.0 / D, EPS, ALU.mult, ALU.add)
                    pool.drain()
                    pool.tensor_tensor(rstd[:, r], meansq[:, r], minus_half[:, :], ALU.pow)\
                        .then_inc(s_rstd, 1)

            with pool.Fori(0, QK_BLOCKS // 2) as i:
                units(i)
            pool.wait_ge(s_blank, 1)
            gather(0, 0)
            pool.wait_ge(s_v[0], 16 * (NCH - 1))
            gather(1, 1)

            def tile(t):
                for n in range(TP):
                    p, r = TP * t + n, n % 4
                    m = n // HK + 1
                    fetch = n % HK == HK // 2 and not (isinstance(t, int) and TB * t + m in (0, 1, NB))
                    if fetch:
                        pool.wait_ge(s_pv, HK * (TB * t + m - 1))
                        pool.wait_ge(s_v[(m + 1) % 2],
                                     16 * (NCH - 1) * (2 * t + (m + 1) // 2))
                    pool.wait_ge(s_inv, p + 1)
                    pool.tensor_tensor(probs[:, r, 0:KEYS], probs[:, r, 0:KEYS],
                                       inverse[:, r:r + 1].to_broadcast([P, KEYS]), ALU.mult)\
                        .then_inc(s_norm, 1)
                    if fetch:
                        gather(TB * t + m, m % 2)

            tile(0)
            with pool.Fori(1, NT - 1) as t:
                tile(t)
            tile(NT - 1)

        @block.scalar
        def _(act):
            act.wait_ge(s_angle, 1)
            act.activation(straight[:, 0], reduced[0], ACT.Sin).then_inc(s_trig, 1)
            act.activation(straight[:, 1], reduced[1], ACT.Sin).then_inc(s_trig, 1)
            act.activation(straight[:, 2], reduced[1], ACT.Sin, scale=-1.0).then_inc(s_trig, 1)

            def split_w(j, c, landed):
                act.wait_ge(s_wraw[c], 16 * landed)
                if after_start(NT * (j - 1)):
                    act.wait_ge(s_proj, NT * (j - 1))
                act.activation(w_hi[:, c], w_raw[:, c], ACT.Copy).then_inc(s_whi, 1)

            for t in range(NT):
                act.wait_ge(s_x1turn, t + 1)
                act.activation(x1t_hi[:, :, t * P:(t + 1) * P],
                               x1t_ps[:, :].rearrange("p (c n) -> p c n", c=KC), ACT.Copy)\
                   .then_inc(s_x1hi, 1)
                if t == 0:
                    split_w(0, 0, 1)

            def scale(u, n):
                act.wait_ge(s_rstd, u + 1)
                if after_start(u - 1):
                    act.wait_ge(s_turned, u - 1)
                for g in range(G):
                    last = act.activation(rotated[:, n % 2, g * D:(g + 1) * D],
                                          straight[:, n % 4, g * D:(g + 1) * D], ACT.Copy,
                                          scale=rstd[:, n % 4, g:g + 1])
                last.then_inc(s_scaled, 1)

            def stage(u, n, rounds):
                if after_start(rounds):
                    act.wait_ge(s_stored[n % 2], 16 * rounds)
                act.wait_ge(s_turned, u + 1)
                act.activation(staged[:, n % 2].rearrange("d (b g s) -> d g b s", b=TB, g=G),
                               turn_ps[n % 2][:, :].rearrange("d (g b s) -> d g b s", b=TB, g=G),
                               ACT.Copy).then_inc(s_staged, 1)

            def units(i):
                first, last = isinstance(i, int) and i == 0, isinstance(i, int) and i == QK_BLOCKS // 2
                for n in range(BODY):
                    u = BODY * i + n
                    if n == 2:
                        split_w(2 * i + 1, 1, i + 1)
                    if n == NT + 2 and not last:
                        split_w(2 * i + 2, 0, i + 2)
                    if last and n < 4:
                        if n < 2:
                            scale(u - 2, n - 2)
                        for m in ((n,), (n,), (2, 3), ())[n]:
                            stage(BODY * i + m - 4, m - 4, NT * i + (m - 4) // 2)
                    act.wait_ge(s_proj, u + 1)
                    if last:
                        if n >= 2:
                            act.wait_ge(s_vstored[n % 2], 16 * (n // 2))
                        else:
                            act.wait_ge(s_sumsq, u - 1)
                        act.activation(square[:, n % 2], proj_ps[n % 2][:, :], ACT.Copy)\
                           .then_inc(s_square, 1)
                    else:
                        if after_start(u - 1):
                            act.wait_ge(s_sumsq, u - 1)
                        act.activation(square[:, n % 2], proj_ps[n % 2][:, :], ACT.Square)\
                           .then_inc(s_square, 1)
                    if not (first and n < 2) and not last:
                        scale(u - 2, n - 2)
                    if not (first and n < 4) and not last:
                        stage(u - 4, n - 4, NT * i + (n - 4) // 2)

            units(0)
            with act.Fori(1, QK_BLOCKS // 2) as i:
                units(i)
            units(QK_BLOCKS // 2)

            def slot(p, n, do_exp, do_copy):
                if do_copy:
                    act.wait_ge(s_pt, p - 1)
                    if after_start(p - 3):
                        act.wait_ge(s_pv, p - 3)
                    act.activation(probs_t[:, n % 2, 0:L], pt_ps[n % 2][:, :], ACT.Copy)\
                       .then_inc(s_ptc, 1)
                if do_exp:
                    act.wait_ge(s_low, p + 1)
                    act.activation(probs[:, n % 4, 0:KEYS], probs[:, n % 4, 0:KEYS], ACT.Exp,
                                   bias=low[:, n % 4:n % 4 + 1], scale=-1.0,
                                   accum_out=total[:, n % 4:n % 4 + 1]).then_inc(s_exp, 1)

            def gap(t):
                act.wait_ge(s_gap, t + 1)
                act.activation(gate[:, 1:2], gate[:, 0:1], ACT.Exp).then_inc(s_gexp, 1)

            for n in range(TP):
                slot(n, n, True, n >= 2)
            with act.Fori(1, NT) as t:
                for n in range(TP):
                    slot(TP * t + n, n, True, True)
                    if n == 10:
                        gap(t - 1)
            for n in range(2):
                slot(PAIRS + n, n, False, True)
            gap(NT - 1)

        @block.tensor
        def _(pe):
            pe.wait_ge(s_const, 16 * N_CONST)
            def turn_x1(t):
                pe.wait_ge(s_x1, t + 1)
                if t >= 1:
                    pe.wait_ge(s_x1lo, t)
                for k in range(KC):
                    last = pe.transpose(x1t_ps[:, k * P:(k + 1) * P], x1[:, t % 2, k * P:(k + 1) * P],
                                        ident)
                last.then_inc(s_x1turn, 1)

            for t in range(NT):
                c = t % 2
                pe.wait_ge(s_l0in[c], 16 * (TB + 2) * (t // 2 + 1))
                if t >= 2:
                    pe.wait_ge(s_x1, t - 1)
                for k in range(KC):
                    for b in range(TB):
                        last = pe.matmul(l0_ps[c][SEQ * b:SEQ * b + SEQ, :],
                                         x0t[:, c, k, SEQ * b:SEQ * b + SEQ], w0_sb[:, c, b, k, :],
                                         start=(k == 0), stop=(k == KC - 1))
                last.then_inc(s_l0, 1)
                if t >= 1:
                    turn_x1(t - 1)
            turn_x1(NT - 1)
            pe.wait_ge(s_x1lo, NT)

            def project(u, n):
                t, c = n % NT, n // NT
                for k in range(KC):
                    xs, ws = slice(t * P, (t + 1) * P), slice(k * HID, (k + 1) * HID)
                    for a, w in ((x1t_hi, w_hi), (x1t_hi, w_lo), (x1t_lo, w_hi)):
                        last = pe.matmul(proj_ps[n % 2][:, :], a[:, k, xs], w[:, c, ws],
                                         start=(k == 0 and w is w_hi and a is x1t_hi),
                                         stop=(k == KC - 1 and a is x1t_lo))
                last.then_inc(s_proj, 1)

            def turn(u, n):
                pe.wait_ge(s_scaled, u + 1)
                if after_start(u - 1):
                    pe.wait_ge(s_staged, u - 1)
                for g in range(G):
                    last = pe.transpose(turn_ps[n % 2][:, g * P:(g + 1) * P],
                                        rotated[:, n % 2, g * D:(g + 1) * D], ident)
                last.then_inc(s_turned, 1)

            def units(i):
                first, last = isinstance(i, int) and i == 0, isinstance(i, int) and i == QK_BLOCKS // 2
                for n in range(BODY):
                    u = BODY * i + n
                    if n % NT == 0:
                        pe.wait_ge(s_wlo, 2 * i + n // NT + 1)
                    if after_start(u - 1):
                        if last and n >= 2:
                            pe.wait_ge(s_square, u - 1)
                        else:
                            pe.wait_ge(s_cross, u - 1)
                    project(u, n)
                    if not (first and n < 3) and not (last and n >= 3):
                        turn(u - 3, n - 3)

            units(0)
            with pe.Fori(1, QK_BLOCKS // 2) as i:
                units(i)
            units(QK_BLOCKS // 2)

            def scores(p, n, arrived):
                hk, c = n % HK, n // HK % 2
                if hk == 0:
                    pe.wait_ge(s_k[c], 16 * K_DMAS * arrived)
                if after_start(p):
                    pe.wait_ge(s_low, p)
                q = qk_sb[:, c, hk * P:(hk + 1) * P]
                pe.matmul(s_ps[:, 0:L].rearrange("p (a b) -> p a b", b=PSIZE), q,
                          kt[:, c, :, hk * PSIZE:(hk + 1) * PSIZE], start=True, stop=True)
                new = Q_COLS + hk * SEQ
                pe.matmul(s_ps[:, L:L + P], q, qk_sb[:, c, new:new + P], start=True, stop=True)\
                  .then_inc(s_scores, 1)

            def turn_probs(p, n):
                pe.wait_ge(s_norm, p + 1)
                if after_start(p - 1):
                    pe.wait_ge(s_ptc, p - 1)
                    pe.wait_ge(s_pnc, p - 1)
                for j in range(NCH - 1):
                    pe.transpose(pt_ps[n % 2][:, j * P:(j + 1) * P], probs[:, n % 4, j * P:(j + 1) * P],
                                 ident)
                pe.transpose(pn_ps[n % 2][:, 0:P], probs[:, n % 4, L:L + P], ident).then_inc(s_pt, 1)

            def values(p, n, arrived):
                hk, c = n % HK, n // HK % 2
                if hk == 0:
                    pe.wait_ge(s_v[c], 16 * (NCH - 1) * arrived)
                    pe.wait_ge(s_vnew[c], 16 * arrived)
                pe.wait_ge(s_ptc, p + 1)
                pe.wait_ge(s_pnc, p + 1)
                if after_start(p):
                    pe.wait_ge(s_o, p)
                for j in range(NCH):
                    last = pe.matmul(o_ps[:, 0:P], vt[:, c, j, hk * D:(hk + 1) * D],
                                     probs_t[:, n % 2, j * P:(j + 1) * P],
                                     start=(j == 0), stop=(j == NCH - 1))
                last.then_inc(s_pv, 1)

            def tail(t, n):
                if n == 3:
                    if isinstance(t, int) and t == 0 or not isinstance(t, int):
                        pe.wait_ge(s_weights, 16 * 4)
                    if after_start(t):
                        pe.wait_ge(s_final, t)
                    pe.wait_ge(s_o, TP * (t + 1))
                    for h in range(HQ):
                        last = pe.matmul(acc[:, :], o_t[:, h, :], wo_sb[:, h, :], start=(h == 0),
                                         stop=(h == HQ - 1))
                    last.then_inc(s_wo, 1)
                if n == 5:
                    pe.wait_ge(s_tail_in, 16 * (TB + 1) * (t + 1))
                    pe.wait_ge(s_res2, t + 1)
                    pe.matmul(acc[:, :], w2_sb[:, :], res2[:, :], start=True, stop=True).then_inc(s_l2, 1)
                if n == 7:
                    pe.wait_ge(s_res3, t + 1)
                    for k in range(KC):
                        last = pe.transpose(acc[:, k * P:(k + 1) * P], res3[:, k * P:(k + 1) * P], ident)
                    last.then_inc(s_r3turn, 1)
                if n == 9:
                    pe.wait_ge(s_r3t, t + 1)
                    for k in range(KC):
                        last = pe.matmul(acc[:, 0:ER + E], res3_t[:, k, :], a3_sb[:, k, :],
                                         start=(k == 0), stop=(k == KC - 1))
                    last.then_inc(s_hid, 1)
                if n == 14:
                    pe.wait_ge(s_gated, t + 1)
                    pe.transpose(acc[:, 0:P], gated, ident).then_inc(s_gturn, 1)
                if n == 16:
                    pe.wait_ge(s_gt, t + 1)
                    for k in range(KC):
                        pe.matmul(acc[:, :], res3_t[:, k, :], w3_sb[:, k, :], start=(k == 0), stop=False)
                    pe.matmul(acc[:, :], gated_t[:, :], b3_sb[:, :], start=False, stop=True)\
                      .then_inc(s_l3, 1)

            def slot(t, n, do_scores, do_turn, do_values, do_tail):
                p = TP * t + n
                if do_scores:
                    scores(p, n, 2 * t + n // HK // 2 + 1)
                if do_turn:
                    turn_probs(p - 2, n - 2)
                if do_tail:
                    tail(t - 1, n)
                if do_values:
                    values(p - 3, (n - 3) % TP, 2 * t + (n - 3) // (2 * HK) + 1)

            for n in range(TP):
                slot(0, n, True, n >= 2, n >= 3, False)
            with pe.Fori(1, NT) as t:
                for n in range(TP):
                    slot(t, n, True, True, True, True)
            for n in range(17):
                slot(NT, n, False, n < 2, n < 3, True)

        @block.vector
        def _(dve):
            dve.wait_ge(s_const, 16 * N_CONST)
            dve.tensor_copy(lens_f[:, :], lens_all[:, :])
            dve.drain()
            for g in range(TB):
                q = slice(SEQ * g, SEQ * g + SEQ)
                dve.tensor_scalar(v_rows[q, :], pages_all[q, g::TB], float(PSIZE), token_no[q], ALU.mult,
                                  ALU.add)
                dve.tensor_scalar(pos[q, :], lens_f[q, g::TB], token_no[q], None, ALU.add)
                dve.tensor_copy(lang_f[q, :], lang_all[q, g::TB])
            dve.drain()
            for t in range(NT):
                dve.tensor_scalar(lang_bias[:, t], expert_no, lang_f[:, t:t + 1], LANG_BIAS, ALU.is_equal,
                                  ALU.mult)
                dve.tensor_scalar(angle[:, t * D // 2:(t + 1) * D // 2], freq, pos[:, t:t + 1], None,
                                  ALU.mult)
            for way, (turn, shift) in enumerate(((0.25, np.pi / 2), (0.0, 0.0))):
                dve.drain()
                dve.tensor_scalar(turns, angle, 1.0 / (2 * np.pi), turn, ALU.mult, ALU.add)
                dve.drain()
                dve.tensor_scalar(turns, turns, ROUND, None, ALU.add)
                dve.drain()
                dve.tensor_scalar(turns, turns, -ROUND, None, ALU.add)
                dve.drain()
                dve.scalar_tensor_tensor(out=reduced[way], in0=turns, scalar=-TURN_A, in1=angle,
                                         op0=ALU.mult, op1=ALU.add)
                for part in (TURN_B, TURN_C):
                    dve.drain()
                    dve.scalar_tensor_tensor(out=reduced[way], in0=turns, scalar=-part, in1=reduced[way],
                                             op0=ALU.mult, op1=ALU.add)
                dve.drain()
                dve.tensor_scalar(reduced[way], reduced[way], float(shift), SIN_LIMIT, ALU.add, ALU.min)
                dve.drain()
                last = dve.tensor_scalar(reduced[way], reduced[way], -SIN_LIMIT, None, ALU.max)
            last.then_inc(s_angle, 1)
            dve.wait_ge(s_trig, 3)
            H = D // 2
            for w in range(2):
                for half in range(2):
                    here, other = (qk_w[:, w, x * H:(x + 1) * H].unsqueeze(1).to_broadcast([P, NT, H])
                                   for x in (half, 1 - half))
                    cosine, sine = (straight[:, x].rearrange("p (t f) -> p t f", f=H)
                                    for x in (0, 1 if half else 2))
                    dve.tensor_tensor(table[:, 2 * w, :, half * H:(half + 1) * H], cosine, here, ALU.mult)
                    last = dve.tensor_tensor(table[:, 2 * w + 1, :, half * H:(half + 1) * H], sine, other,
                                             ALU.mult)
            last.then_inc(s_table, 1)
            dve.wait_ge(s_table, 1)

            def split_w(j, c):
                dve.wait_ge(s_whi, j + 1)
                dve.tensor_tensor(w_lo[:, c], w_raw[:, c], w_hi[:, c].bitcast(F32), ALU.subtract)\
                   .then_inc(s_wlo, 1)

            for t in range(NT):
                c = t % 2
                dve.wait_ge(s_l0, t + 1)
                if t >= 2:
                    dve.wait_ge(s_x1out, 16 * (t - 1))
                    dve.wait_ge(s_x1turn, t - 1)
                dve.tensor_tensor(x1[:, c], l0_ps[c][:, :], x0[:, c], ALU.add).then_inc(s_x1, 1)
                dve.wait_ge(s_x1hi, t + 1)
                xs = slice(t * P, (t + 1) * P)
                dve.tensor_tensor(x1t_lo[:, :, xs], x1t_ps[:, :].rearrange("p (c n) -> p c n", c=KC),
                                  x1t_hi[:, :, xs].bitcast(F32), ALU.subtract).then_inc(s_x1lo, 1)
                if t == 0:
                    split_w(0, 0)

            def units(i, w):
                for n in range(BODY):
                    u, t = BODY * i + n, n % NT
                    if n == 4:
                        split_w(2 * i + 1, 1)
                    if n == NT + 4:
                        split_w(2 * i + 2, 0)
                    both = proj_ps[n % 2][:, :].rearrange("p (g h f) -> p g h f", g=G, h=2)
                    dve.wait_ge(s_square, u + 1)
                    if after_start(u - 3):
                        dve.wait_ge(s_scaled, u - 3)
                    dve.tensor_tensor(straight[:, n % 4].rearrange("p (g d) -> p g d", g=G),
                                      proj_ps[n % 2][:, :].rearrange("p (g d) -> p g d", g=G),
                                      table[:, 2 * w, t:t + 1, :].to_broadcast([P, G, D]), ALU.mult)
                    if after_start(u - 1):
                        dve.wait_ge(s_rot, u - 1)
                    swapped = crossed[:, n % 2].rearrange("p (g h f) -> p g h f", g=G, h=2)
                    for half in range(2):
                        last = dve.tensor_tensor(
                            swapped[:, :, half, :], both[:, :, 1 - half, :],
                            table[:, 2 * w + 1, t:t + 1, half * H:(half + 1) * H].to_broadcast([P, G, H]),
                            ALU.mult)
                    last.then_inc(s_cross, 1)
                    dve.tensor_reduce(sumsq[:, n % 4], square[:, n % 2].rearrange("p (g d) -> p g d", g=G),
                                      AX_X, ALU.add).then_inc(s_sumsq, 1)

            units(0, 0)
            with dve.Fori(1, Q_BLOCKS // 2) as i:
                units(i, 0)
            units(Q_BLOCKS // 2, 1)
            dve.wait_ge(s_proj, QK_UNITS + 4)
            split_w(QKV_BLOCKS - 1, 1)

            for c in range(2):
                dve.wait_ge(s_stored[c], 16 * QK_UNITS // 2)
                dve.wait_ge(s_vstored[c], 16 * (UNITS - QK_UNITS) // 2)
            dve.wait_ge(s_x1out, 16 * NT)
            dve.memset(vt[SEQ:2 * SEQ, :, NCH - 1], 0.0)
            dve.memset(vt[2 * SEQ:P, :, NCH - 1], 0.0)
            dve.memset(qk_sb[:, :, QK_ROW:], 0.0)
            dve.memset(probs[:, :, KEYS:], 0.0)
            dve.memset(mask[:, L:], 0.0)
            dve.memset(w2_sb[:, :], 0.0)
            dve.drain()
            dve.memset(top[:, :], 0.0).then_inc(s_blank, 1)

            def slot(t, n, do_pair, do_inverse, do_new, do_o):
                p = TP * t + n
                if do_inverse:
                    dve.wait_ge(s_exp, p)
                if do_pair:
                    dve.wait_ge(s_scores, p + 1)
                if do_inverse:
                    dve.reciprocal(inverse[:, (n - 1) % 4:(n - 1) % 4 + 1],
                                   total[:, (n - 1) % 4:(n - 1) % 4 + 1]).then_inc(s_inv, 1)
                if do_pair and n % HK == 0:
                    b = TB * t + n // HK
                    dve.tensor_scalar(mask[:, 0:L], key_no, lens_f[:, bass.ds(b, 1)], MASKED, ALU.is_ge,
                                      ALU.mult)
                    dve.drain()
                if do_pair:
                    dve.tensor_tensor_reduce(probs[:, n % 4, 0:KEYS], s_ps[:, 0:KEYS], mask[:, :], -SCALE,
                                             3e38, ALU.add, ALU.min, low[:, n % 4:n % 4 + 1])\
                       .then_inc(s_low, 1)
                if do_new:
                    dve.wait_ge(s_pt, p - 1)
                    if after_start(p - 3):
                        dve.wait_ge(s_pv, p - 3)
                    dve.tensor_copy(probs_t[:, n % 2, L:L + P], pn_ps[n % 2][:, 0:P]).then_inc(s_pnc, 1)
                if do_o:
                    k = (n - 3) % TP
                    b, hk = k // HK, k % HK
                    dve.wait_ge(s_pv, p - 2)
                    if k == 0 and not (isinstance(t, int) and t == 0):
                        dve.wait_ge(s_wo, t)
                    dve.tensor_copy(o_t[:, hk * G:(hk + 1) * G, b * SEQ:(b + 1) * SEQ],
                                    o_ps[:, 0:P].rearrange("d (g s) -> d g s", g=G)).then_inc(s_o, 1)

            def tail(t, n):
                if n == 4:
                    dve.wait_ge(s_tail_in, 16 * (TB + 1) * (t + 1))
                    if after_start(t):
                        dve.wait_ge(s_out, 16 * t)
                    dve.wait_ge(s_wo, t + 1)
                    dve.tensor_tensor(res2[:, :], acc[:, :], res1[:, :], ALU.add).then_inc(s_res2, 1)
                if n == 6:
                    dve.wait_ge(s_l2, t + 1)
                    dve.tensor_tensor(res3[:, :], acc[:, :], res2[:, :], ALU.add).then_inc(s_res3, 1)
                if n == 8:
                    dve.wait_ge(s_r3turn, t + 1)
                    dve.tensor_copy(res3_t[:, :, :], acc[:, :].rearrange("p (c n) -> p c n", c=KC))\
                       .then_inc(s_r3t, 1)
                if n == 10:
                    dve.wait_ge(s_hid, t + 1)
                    dve.tensor_copy(hid[:, :], acc[:, 0:ER + E])
                    dve.drain()
                    dve.tensor_tensor(picks[:, 2:3], hid[:, ER:].unsqueeze(1), lang_bias[:, bass.ds(t, 1)],
                                      ALU.add)
                    dve.drain()
                    dve.max(top[:, :], picks[:, 2])
                    dve.drain()
                    dve.max_index(top_at[:, :], top[:, :], picks[:, 2])
                    dve.tensor_tensor(gate[:, 0:1], top[:, 1:2], top[:, 0:1], ALU.subtract)\
                       .then_inc(s_gap, 1)
                if n == 12:
                    dve.wait_ge(s_gexp, t + 1)
                    dve.tensor_copy(gate[:, 5:7], top_at[:, 0:2])
                    dve.tensor_scalar(gate[:, 2:3], gate[:, 1:2], 1.0, None, ALU.add)
                    dve.drain()
                    dve.reciprocal(gate[:, 3:4], gate[:, 2:3])
                    dve.drain()
                    dve.tensor_tensor(gate[:, 4:5], gate[:, 1:2], gate[:, 3:4], ALU.mult)
                    dve.drain()
                    for x in range(2):
                        dve.tensor_scalar(picks[:, x], expert_no, gate[:, 5 + x:6 + x],
                                          gate[:, 3 + x:4 + x], ALU.is_equal, ALU.mult)
                    dve.drain()
                    dve.tensor_tensor(picks[:, 2], picks[:, 0], picks[:, 1], ALU.add)
                    dve.drain()
                    dve.scalar_tensor_tensor(
                        out=gated.rearrange("p (e r) -> p e r", e=E),
                        in0=hid[:, 0:ER].rearrange("p (e r) -> p e r", e=E), scalar=SCALING,
                        in1=picks[:, 2].unsqueeze(2).to_broadcast([P, E, R]), op0=ALU.mult,
                        op1=ALU.mult).then_inc(s_gated, 1)
                if n == 15:
                    dve.wait_ge(s_gturn, t + 1)
                    dve.tensor_copy(gated_t[:, :], acc[:, 0:P]).then_inc(s_gt, 1)
                if n == 18:
                    dve.wait_ge(s_l3, t + 1)
                    dve.tensor_tensor(res2[:, :], acc[:, :], res3[:, :], ALU.add).then_inc(s_final, 1)

            for n in range(TP):
                slot(0, n, True, n >= 1, n >= 2, n >= 3)
            with dve.Fori(1, NT) as t:
                for n in range(TP):
                    slot(t, n, True, True, True, True)
                    tail(t - 1, n)
            for n in range(19):
                slot(NT, n, False, n < 1, n < 2, n < 3)
                tail(NT - 1, n)


def kernel(**inputs):
    import concourse.bacc as bacc
    from concourse.bass_utils import run_bass_kernel_spmd

    def arr(name):
        return np.asarray(inputs[name])

    def feature_chunks(w):
        return w.T.reshape(KC, P, -1).transpose(1, 0, 2)

    x = arr("x").reshape(NB * SEQ, HID)
    w0 = arr("L0_cond_weight")
    qkv = np.concatenate([arr("L1_cond_Wq"), arr("L1_cond_Wk"), arr("L1_cond_Wv")])
    consts = np.zeros((P, C_ALL), np.float32)
    consts[:, C_IDENT:C_IDENT + P] = np.eye(P)
    power = (10000.0 ** (np.arange(0, D, 2) / D)).astype(np.float32)
    consts[:, C_FREQ:C_FREQ + D // 2] = np.float32(1.0) / power
    consts[:, C_KEY:C_KEY + L] = np.arange(L)
    consts[:, C_EXPERT:C_EXPERT + E] = np.arange(E)
    consts[:, C_TOKEN] = np.arange(P) % SEQ
    arrays = {
        "x_tok": x,
        "x_feat": feature_chunks(x),
        "adapter": arr("itok_B_0_15").reshape(1, NB),
        "pages": arr("itok_Bx16_0_63").reshape(1, NB * NPP),
        "lens": arr("itok_B_207_1644").reshape(1, NB),
        "subject": arr("itok_B_0_30").reshape(1, NB),
        "language": arr("itok_B_0_7").reshape(1, NB),
        "w0": w0.transpose(0, 2, 1).reshape(-1, KC, P, HID).transpose(0, 2, 1, 3),
        "wqkv": qkv.reshape(QKV_BLOCKS, HID, KC, P).transpose(0, 3, 2, 1).reshape(QKV_BLOCKS, P, KC * HID),
        "wo": arr("L1_cond_Wo").reshape(HID, HQ, D).transpose(2, 1, 0),
        "kcache": arr("L1_cond_k_cache").transpose(0, 3, 2, 1).reshape(PAGES, D, HK * PSIZE),
        "vcache": arr("L1_cond_v_cache").reshape(PAGES * PSIZE, HK * D),
        "q_w": arr("L1_cond_q_norm_w").reshape(1, D),
        "k_w": arr("L1_cond_k_norm_w").reshape(1, D),
        "w2": arr("L2_cond_weights"),
        "w3": feature_chunks(arr("L3_cond_W")),
        "a3": feature_chunks(np.concatenate([arr("L3_cond_A").reshape(ER, HID), arr("L3_cond_Wr")])),
        "b3": arr("L3_cond_B").transpose(0, 2, 1).reshape(ER, HID),
        "consts": consts,
    }
    arrays = {k: np.ascontiguousarray(v) for k, v in arrays.items()}
    nc = bacc.Bacc("TRN2", target_bir_lowering=False, num_devices=1)
    aps = {k: nc.dram_tensor(k, v.shape, mybir.dt.from_np(v.dtype), kind="ExternalInput").ap()
           for k, v in arrays.items()}
    out = nc.dram_tensor("out", (NB * SEQ, HID), F32, kind="ExternalOutput").ap()
    build(nc, out=out, **aps)
    got = run_bass_kernel_spmd(nc, [arrays], core_ids=[0]).results[0]["out"]
    return got.reshape(NB, SEQ, HID)
```

```python
from contextlib import ExitStack

import numpy as np

import concourse.bass as bass
from concourse import mybir

F32 = mybir.dt.float32
F32R = mybir.dt.float32r
I32 = mybir.dt.int32
U32 = mybir.dt.uint32
ALU = mybir.AluOpType
ACT = mybir.ActivationFunctionType
AX_X = mybir.AxisListType.X
SP_ENGINE = mybir.EngineType.SP

P = 128
NB, SEQ, HID = 32, 32, 512
D, HQ, HK = 128, 32, 8
G = HQ // HK
PAGES, PSIZE, NPP = 64, 32, 16
L = NPP * PSIZE
KEYS = L + SEQ
NCH = L // P + 1
TB = P // SEQ
NT = NB // TB
KC = HID // P
QKV_BLOCKS = (HQ + 2 * HK) * D // HID
QK_BLOCKS = (HQ + HK) * D // HID
Q_BLOCKS = HQ * D // HID
QK_ROW = QK_BLOCKS * P
Q_COLS = Q_BLOCKS * P
SLOTS = NPP + 1
E, R = 8, 16
ER = E * R
SCALE = 1.0 / float(np.sqrt(D))
EPS = 1e-6
RING = 4
LANG_BIAS = 5.0
SCALING = 2.0
MASKED = -1e30

C_IDENT, C_FREQ, C_KEY, C_EXPERT, C_TOKEN = 0, P, P + D // 2, P + D // 2 + L, P + D // 2 + L + E
C_ALL = C_TOKEN + 1

TURN_A = 6.28125
TURN_B = float(np.round((2 * np.pi - TURN_A) * 2.0**21) / 2.0**21)
TURN_C = float(np.float32(2 * np.pi - TURN_A - TURN_B))
ROUND = 1.5 * 2.0**23
SIN_LIMIT = 3.1415925


def after_start(value):
    return not isinstance(value, int) or value > 0


def place(i, n):
    return (n // 2, n % 2) if isinstance(i, int) and i == 0 else (n % NT, n // NT)


def build(nc, x_tok, x_feat, adapter, pages, lens, subject, language, w0, wqkv, wo, kcache, vcache,
          q_w, k_w, w2, w3, a3, b3, consts, out):
    qk_dram = nc.dram_tensor("qk_scratch", (NB, D, QK_ROW), F32).ap()
    v_dram = nc.dram_tensor("v_scratch", (NB * SEQ, HK * D), F32).ap()
    o_dram = nc.dram_tensor("o_scratch", (NB, D, HQ * SEQ), F32).ap()
    x1_dram = nc.dram_tensor("x1_scratch", (NB * SEQ, HID), F32).ap()

    ctx = ExitStack()
    stage_a, stage_b, stage_c = ExitStack(), ExitStack(), ExitStack()
    with ctx:
        def sem(name):
            return ctx.enter_context(nc.semaphore(name))

        def keep(name, shape, dt=F32):
            return ctx.enter_context(nc.sbuf_tensor(name, shape, dt))

        const = keep("const", [P, C_ALL])
        ident = const[:, C_IDENT:C_IDENT + P]
        freq = const[:, C_FREQ:C_FREQ + D // 2]
        key_no = const[:, C_KEY:C_KEY + L]
        expert_no = const[:, C_EXPERT:C_EXPERT + E]
        token_no = const[:, C_TOKEN:C_TOKEN + 1]
        adapter_sb = keep("adapter_sb", [1, NB], I32)
        subject_sb = keep("subject_sb", [1, NB], I32)
        pages_all = keep("pages_all", [P, NB * NPP], I32)
        lens_f = keep("lens_f", [P, NB])
        v_now = keep("v_now", [P, NCH - 1], U32)
        minus_half = keep("minus_half", [P, G])
        v_rows = keep("v_rows", [P, NB * (NCH - 1)], U32)
        lang_bias = keep("lang_bias", [P, NT, E])

        def sa(name, shape, dt=F32):
            return stage_a.enter_context(nc.sbuf_tensor(name, shape, dt))

        def pa(name):
            return stage_a.enter_context(nc.psum_tensor(name, [P, HID], F32))

        w0_sb = sa("w0_sb", [P, 2, TB, KC, HID])
        x0t = sa("x0t", [P, 2, KC, P])
        x0 = sa("x0", [P, 2, HID])
        x1 = sa("x1", [P, 2, HID])
        w_raw = sa("w_raw", [P, 2, KC * HID])
        straight = sa("straight", [P, 4, HID])
        crossed = sa("crossed", [P, 2, HID])
        rotated = sa("rotated", [P, 2, HID])
        staged = sa("staged", [P, RING, HID])
        sumsq = sa("sumsq", [P, 4, G])
        meansq = sa("meansq", [P, 4, G])
        rstd = sa("rstd", [P, 4, G])
        qk_w = sa("qk_w", [P, 2, D])
        pos = sa("pos", [P, NT])
        lang_f = sa("lang_f", [P, NT])
        lens_all = sa("lens_all", [P, NB], I32)
        lang_all = sa("lang_all", [P, NB], I32)
        table = sa("table", [P, 4, NT, D])
        square = sa("square", [P, 2, HID])
        x1t_hi = sa("x1t_hi", [P, KC, NT * P], F32R)
        x1t_lo = sa("x1t_lo", [P, KC, NT * P], F32R)
        w_hi = sa("w_hi", [P, 2, KC * HID], F32R)
        w_lo = sa("w_lo", [P, 2, KC * HID], F32R)
        angle, turns = square[:, 0, :], square[:, 1, :]
        reduced = [crossed[:, i, :] for i in range(2)]
        l0_ps = [pa(f"l0_ps{i}") for i in range(2)]
        turn_ps = [pa(f"turn_ps{i}") for i in range(2)]
        x1t_ps, _ = pa("x1t_ps"), pa("unused_ps")
        proj_ps = [pa(f"proj_ps{i}") for i in range(2)]
        stage_a.close()

        def sb(name, shape, dt=F32):
            return stage_b.enter_context(nc.sbuf_tensor(name, shape, dt))

        kt = sb("kt", [P, 2, SLOTS, HK * PSIZE])
        vt = sb("vt", [P, 2, NCH, HK * D])
        q_raw = sb("q_raw", [P, 2, Q_COLS])
        q_hi = sb("q_hi", [P, 2, Q_COLS], F32R)
        q_lo = sb("q_lo", [P, 2, Q_COLS], F32R)
        k_hi = sb("k_hi", [P, 4, KEYS], F32R)
        k_lo = sb("k_lo", [P, 4, KEYS], F32R)
        probs = sb("probs", [P, 4, NCH * P])
        mask = sb("mask", [P, 2, KEYS])
        low = sb("low", [P, 4])
        total = sb("total", [P, 4])
        inverse = sb("inverse", [P, 4])
        probs_t = sb("probs_t", [P, 2, NCH * P])
        o_sb = sb("o_sb", [P, 2, HK, P])
        s_ps = stage_b.enter_context(nc.psum_tensor("s_ps", [P, 2 * HID], F32))
        pt_ps = [stage_b.enter_context(nc.psum_tensor(f"pt_ps{i}", [P, 2 * HID], F32)) for i in range(2)]
        o_ps = [stage_b.enter_context(nc.psum_tensor(f"o_ps{i}", [P, HID], F32)) for i in range(2)]
        stage_b.close()
        SPLIT = (SLOTS + 1) // 2 * PSIZE
        scores_ps = s_ps[:, HID - SPLIT:HID - SPLIT + KEYS]

        def sc(name, shape, dt=F32):
            return stage_c.enter_context(nc.sbuf_tensor(name, shape, dt))

        o_raw = [sc(f"o_raw{i}", [P, NB, P]) for i in range(2)]
        wo_hi = sc("wo_hi", [P, 2, HID], F32R)
        wo_raw0 = sc("wo_raw0", [P, G, HID])
        o_hi = sc("o_hi", [P, 2, NB * SEQ], F32R)
        o_lo = sc("o_lo", [P, 2, NB * SEQ], F32R)
        wo_raw = [wo_raw0, sc("wo_raw1", [P, G, HID])]
        wo_lo = sc("wo_lo", [P, 2, HID], F32R)
        w3_sb = sc("w3_sb", [P, KC, HID])
        a3_sb = sc("a3_sb", [P, KC, ER + E])
        b3_sb = sc("b3_sb", [P, HID])
        w2_sb = sc("w2_sb", [P, NT, P])
        res1 = sc("res1", [P, NT, HID])
        res2 = sc("res2", [P, NT, HID])
        res3 = sc("res3", [P, NT, HID])
        r3t = sc("r3t", [P, NT, KC, P])
        hid = sc("hid", [P, NT, ER + E])
        gated_t = sc("gated_t", [P, NT, P])
        logits = sc("logits", [P, NT, E])
        top = sc("top", [P, NT, 8])
        top_at = sc("top_at", [P, NT, 8], U32)
        gate = sc("gate", [P, 6, NT])
        picks = sc("picks", [P, 2, NT, E])
        top_f = sc("top_f", [P, NT, 8])
        acc = [stage_c.enter_context(nc.psum_tensor(f"acc{i}", [P, HID], F32)) for i in range(NT)]
        stage_c.close()

        def gated_ps(t):
            return acc[NT - 2 + t // 4][:, t % 4 * P:(t % 4 + 1) * P]

        s_const = sem("s_const")
        s_l0in = [sem(f"s_l0in{i}") for i in range(2)]
        s_x1out = [sem(f"s_x1out{i}") for i in range(2)]
        s_wraw = [sem(f"s_wraw{i}") for i in range(2)]
        s_stored = [sem(f"s_stored{i}") for i in range(RING)]
        s_meansq = sem("s_meansq")
        s_vstored = [sem(f"s_vstored{i}") for i in range(2)]
        s_index = sem("s_index")
        s_table = sem("s_table")
        s_angle = sem("s_angle")
        s_trig = sem("s_trig")
        s_l0 = sem("s_l0")
        s_x1 = sem("s_x1")
        s_x1turn = sem("s_x1turn")
        s_x1hi = sem("s_x1hi")
        s_x1lo = sem("s_x1lo")
        s_whi = sem("s_whi")
        s_wlo = sem("s_wlo")
        s_proj = sem("s_proj")
        s_square = sem("s_square")
        s_cross = sem("s_cross")
        s_sumsq = sem("s_sumsq")
        s_rstd = sem("s_rstd")
        s_rot = sem("s_rot")
        s_scaled = sem("s_scaled")
        s_turned = sem("s_turned")
        s_staged = sem("s_staged")

        s_blank = sem("s_blank")
        s_q = [sem(f"s_q{i}") for i in range(2)]
        s_k = [sem(f"s_k{i}") for i in range(2)]
        s_vnew = [sem(f"s_vnew{i}") for i in range(2)]
        s_v = [sem(f"s_v{i}") for i in range(2)]
        s_khi = sem("s_khi")
        s_klo = sem("s_klo")
        s_qhi = sem("s_qhi")
        s_qlo = sem("s_qlo")
        s_scores = sem("s_scores")
        s_low = sem("s_low")
        s_exp = sem("s_exp")
        s_inv = sem("s_inv")
        s_norm = sem("s_norm")
        s_pt = sem("s_pt")
        s_ptc = sem("s_ptc")
        s_pv = sem("s_pv")
        s_o = sem("s_o")
        s_ostored = [sem(f"s_ostored{i}") for i in range(2)]

        s_late = sem("s_late")
        s_late2 = sem("s_late2")
        s_w2blank = sem("s_w2blank")
        s_oin = [sem(f"s_oin{i}") for i in range(2)]
        s_ohi = sem("s_ohi")
        s_olo = sem("s_olo")
        s_wo = sem("s_wo")
        s_acc = sem("s_acc")
        s_res2 = sem("s_res2")
        s_l2 = sem("s_l2")
        s_res3 = sem("s_res3")
        s_r3turn = sem("s_r3turn")
        s_r3t = sem("s_r3t")
        s_hid = sem("s_hid")
        s_hidc = sem("s_hidc")
        s_gap = sem("s_gap")
        s_gexp = sem("s_gexp")
        s_gated = sem("s_gated")
        s_gturn = sem("s_gturn")
        s_gt = sem("s_gt")
        s_l3 = sem("s_l3")
        s_final = sem("s_final")
        s_out = sem("s_out")

        N_CONST = 8
        QK_UNITS, UNITS = QK_BLOCKS * NT, QKV_BLOCKS * NT
        BODY = 2 * NT
        PAIRS, TP = NB * HK, TB * HK
        K_DMAS = NPP + 1
        Q_SPLITS = (3, 4)
        HEADS = 2 * G

        def last_sequence(t, n):
            return isinstance(t, int) and TB * t + n // HK + 1 >= NB

        block = ctx.enter_context(nc.Block())

        @block.sync
        def _(sp):
            sp.dma_start(adapter_sb[:, :], adapter).then_inc(s_const, 16)
            sp.dma_start(subject_sb[:, :], subject).then_inc(s_const, 16)
            sp.dma_start(const[:, :], consts).then_inc(s_const, 16)
            sp.dma_start(lens_all[:, :], lens.partition_broadcast(P)).then_inc(s_const, 16)
            sp.dma_start(pages_all[:, :], pages.partition_broadcast(P)).then_inc(s_const, 16)
            sp.dma_start(lang_all[:, :], language.partition_broadcast(P)).then_inc(s_const, 16)
            sp.dma_start(qk_w[:, 0, :], q_w.partition_broadcast(P)).then_inc(s_const, 16)
            sp.dma_start(qk_w[:, 1, :], k_w.partition_broadcast(P)).then_inc(s_const, 16)
            sp.wait_ge(s_const, 16 * N_CONST)

            def load_w(j, c):
                if not isinstance(j, int) or j >= 2:
                    sp.wait_ge(s_wlo, j - 1)
                sp.dma_start(w_raw[:, c:c + 1], wqkv[bass.ds(j, 1)].rearrange("o p n -> p o n"))\
                  .then_inc(s_wraw[c], 16)

            def load_pages(b, c, with_new=False):
                _, page = nc.values_load_multi_w_load_instructions(
                    pages_all[0:1, bass.ds(b * NPP, NPP)], engines=[SP_ENGINE], min_val=0,
                    max_val=PAGES - 1)
                if with_new:
                    load_new(b, c)
                for j in range(NPP):
                    sp.dma_start(kt[:, c, j], kcache[bass.ds(page[j], 1)].rearrange("o d n -> (o d) n"))\
                      .then_inc(s_k[c], 16)

            def load_new(b, c):
                qk = qk_dram[bass.ds(b, 1)].rearrange("o d n -> (o d) n")
                sp.dma_start(q_raw[:, c], qk[:, 0:Q_COLS]).then_inc(s_q[c], 16)
                sp.dma_start(kt[:, c, NPP], qk[:, Q_COLS:]).then_inc(s_k[c], 16)

            def store(i, n):
                (t, half), r = place(i, n), n % RING
                sp.wait_ge(s_staged, BODY * i + n + 1)
                dst = qk_dram[TB * t:TB * t + TB, :, bass.ds((2 * i + half) * P, P)]
                sp.dma_start(dst.rearrange("b d n -> d b n"),
                             staged[:, r].rearrange("d (b n) -> d b n", b=TB))\
                  .then_inc(s_stored[r], 16)

            LAG = 10
            for t in range(NT):
                c = t % 2
                for n in range(max(2 * t - LAG, 0), max(2 * t + 2 - LAG, 0)):
                    store(0, n)
                if t >= 2:
                    sp.wait_ge(s_l0, t - 1)
                    sp.wait_ge(s_x1, t - 1)
                sp.dma_start(x0t[:, c], x_feat[:, :, t * P:(t + 1) * P]).then_inc(s_l0in[c], 16)
                sp.dma_start(x0[:, c], x_tok[t * P:(t + 1) * P, :]).then_inc(s_l0in[c], 16)
                for b in range(TB):
                    a = sp.value_load(adapter_sb[0:1, TB * t + b:TB * t + b + 1], min_val=0,
                                      max_val=w0.shape[0] - 1)
                    sp.dma_start(w0_sb[:, c, b], w0[bass.ds(a, 1)].rearrange("o p c n -> (o p) c n"))\
                      .then_inc(s_l0in[c], 16)
                if t == 0:
                    load_w(0, 0)
                    load_w(1, 1)
                if t >= 1:
                    sp.wait_ge(s_x1, t)
                    sp.dma_start(x1_dram[(t - 1) * P:t * P, :], x1[:, (t - 1) % 2])\
                      .then_inc(s_x1out[(t - 1) % 2], 16)
            load_w(2, 0)
            load_w(3, 1)
            for n in range(2 * NT - LAG, 2 * NT + 2 - LAG):
                store(0, n)
            sp.wait_ge(s_x1, NT)
            sp.dma_start(x1_dram[(NT - 1) * P:NT * P, :], x1[:, (NT - 1) % 2])\
              .then_inc(s_x1out[(NT - 1) % 2], 16)
            for n in range(2 * NT + 2 - LAG, 2 * NT):
                store(0, n)


            def units(i):
                for n in range(BODY):
                    store(i, n)
                    if n == 1:
                        load_w(2 * i + 2, 0)
                    if n == NT + 1:
                        load_w(2 * i + 3, 1)
                    if isinstance(i, int) and n in (2, NT + 2):
                        load_pages(n // NT, n // NT)

            units(1)
            with sp.Fori(2, QK_BLOCKS // 2) as i:
                units(i)

            def load_new_v(b, c):
                sp.dma_start(vt[0:SEQ, c, NCH - 1], v_dram[bass.ds(b * SEQ, SEQ), :]).then_inc(s_vnew[c], 16)

            for u in range(QK_UNITS, UNITS):
                t, h, c = u % NT, u // NT - QK_BLOCKS, u % 2
                sp.wait_ge(s_square, u + 1)
                sp.dma_start(v_dram[t * P:(t + 1) * P, h * HID:(h + 1) * HID], square[:, c])\
                  .then_inc(s_vstored[c], 16)
                if u == QK_UNITS + 4:
                    for r in range(RING):
                        sp.wait_ge(s_stored[r], 16 * QK_UNITS // RING)
                    sp.wait_ge(s_wlo, QKV_BLOCKS)
                    load_new(0, 0)
                    load_new(1, 1)
            for c in range(2):
                sp.wait_ge(s_vstored[c], 16 * (UNITS - QK_UNITS) // 2)
            load_new_v(0, 0)
            load_new_v(1, 1)

            def store_o(b, c):
                sp.wait_ge(s_o, HK * (b + 1))
                sp.dma_start(o_dram[bass.ds(b, 1)].rearrange("o d n -> (o d) n"),
                             o_sb[:, c].rearrange("d k n -> d (k n)")).then_inc(s_ostored[c], 16)

            def tile(t):
                for m in range(TB):
                    b, c = TB * t + m, m % 2
                    if isinstance(t, int) and b < 2:
                        continue
                    sp.wait_ge(s_klo, HK * (b - 1))
                    load_pages(b, c, with_new=True)
                    store_o(b - 2, c)
                    sp.wait_ge(s_pv, HK * (b - 1))
                    load_new_v(b, c)

            tile(0)
            with sp.Fori(1, NT) as t:
                tile(t)

            def load_wo(k, c):
                sp.dma_start(wo_raw[c][:, :, :], wo[:, bass.ds(k * G, G), :]).then_inc(s_oin[c], 16)

            def load_heads(k, c):
                sp.dma_start(o_raw[c][:, :, :], o_dram[:, :, bass.ds(k * P, P)].rearrange("b d n -> d b n"))\
                  .then_inc(s_oin[c], 16)

            b, c = NB - 2, NB % 2
            store_o(b, c)
            sp.wait_ge(s_pv, HK * (b + 1))
            load_wo(0, 0)
            for half in range(2):
                ks = slice(half * HK // 2, (half + 1) * HK // 2)
                sp.wait_ge(s_o, HK * (NB - 1) + ks.stop)
                sp.dma_start(o_dram[NB - 1, :, ks.start * P:ks.stop * P],
                             o_sb[:, 1, ks].rearrange("d k n -> d (k n)")).then_inc(s_ostored[1], 16)
                if half == 0:
                    sp.wait_ge(s_ostored[0], 16 * NB // 2)
                    sp.wait_ge(s_ostored[1], 16 * NB // 2)
                    load_heads(0, 0)
            sp.wait_ge(s_ostored[1], 16 * (NB // 2 + 1))
            load_wo(1, 1)
            load_heads(1, 1)
            sp.dma_start(w3_sb[:, :, :], w3).then_inc(s_late, 16)
            sp.dma_start(a3_sb[:, :, :], a3).then_inc(s_late, 16)
            sp.dma_start(b3_sb[:, :], b3).then_inc(s_late, 16)
            for c in range(2):
                sp.wait_ge(s_x1out[c], 16 * NT // 2)
            sp.dma_start(res1[:, :, :], x1_dram.rearrange("(t p) n -> p t n", p=P)).then_inc(s_late, 16)
            sp.wait_ge(s_w2blank, 1)
            for t in range(NT):
                _, subj = nc.values_load_multi_w_load_instructions(
                    subject_sb[0:1, t * TB:(t + 1) * TB], engines=[SP_ENGINE], min_val=0,
                    max_val=w2.shape[0] - 1)
                for b in range(TB):
                    q = slice(SEQ * b, SEQ * b + SEQ)
                    sp.dma_start(w2_sb[q, t, q], w2[bass.ds(subj[b], 1)].rearrange("o c d -> (o c) d"))\
                      .then_inc(s_late2, 16)
            with sp.Fori(1, HK // 2) as i:
                for c in range(2):
                    sp.wait_ge(s_olo, HEADS * (i - 1) + G * (c + 1))
                    load_wo(2 * i + c, c)
                    load_heads(2 * i + c, c)
            for t in range(NT):
                sp.wait_ge(s_final, t + 1)
                sp.dma_start(out[t * P:(t + 1) * P, :], res1[:, t]).then_inc(s_out, 16)
            sp.wait_ge(s_out, 16 * NT)

        @block.gpsimd
        def _(pool):
            pool.memset(minus_half[:, :], -0.5)

            def rows_of(b):
                pool.tensor_copy(v_now[:, :], v_rows[:, bass.ds(b * (NCH - 1), NCH - 1)])
                pool.drain()

            def gather(c, j):
                pool.indirect_dma_start(vt[:, c, j], None, vcache,
                                        bass.IndirectOffsetOnAxis(ap=v_now[:, j:j + 1], axis=0))\
                    .then_inc(s_v[c], 16)

            def units(i):
                for n in range(BODY):
                    u, c, r = BODY * i + n, n % 2, n % 4
                    pool.wait_ge(s_cross, u + 1)
                    pool.wait_ge(s_sumsq, u + 1)
                    pool.tensor_tensor(straight[:, r], straight[:, r], crossed[:, c], ALU.add)\
                        .then_inc(s_rot, 1)
                    pool.tensor_scalar(meansq[:, r], sumsq[:, r], 1.0 / D, EPS, ALU.mult, ALU.add)\
                        .then_inc(s_meansq, 1)
                    pool.wait_ge(s_meansq, u + 1)
                    pool.tensor_tensor(rstd[:, r], meansq[:, r], minus_half[:, :], ALU.pow)\
                        .then_inc(s_rstd, 1)

            units(0)
            pool.wait_ge(s_index, 1)
            pool.wait_ge(s_x1lo, NT)
            for c in range(2):
                pool.wait_ge(s_x1out[c], 16 * NT // 2)
            for c in range(2):
                if c == 1:
                    pool.wait_ge(s_v[0], 16 * (NCH - 1))
                rows_of(c)
                for j in range(NCH - 1):
                    gather(c, j)
                units(c + 1)
            with pool.Fori(3, QK_BLOCKS // 2) as i:
                units(i)

            def tile(t):
                for n in range(TP):
                    p, r = TP * t + n, n % 4
                    m = n // HK + 1
                    j = n % HK - (HK - NCH + 1)
                    fetch = not (isinstance(t, int) and TB * t + m in (1, NB))
                    if fetch and j == -1:
                        pool.wait_ge(s_v[(m + 1) % 2], 16 * (NCH - 1) * (2 * t + (m + 1) // 2))
                    if fetch and j == 0:
                        pool.wait_ge(s_pv, HK * (TB * t + m - 1))
                    pool.wait_ge(s_inv, p + 1)
                    pool.tensor_tensor(probs[:, r, 0:KEYS], probs[:, r, 0:KEYS],
                                       inverse[:, r:r + 1].to_broadcast([P, KEYS]), ALU.mult)\
                        .then_inc(s_norm, 1)
                    if fetch and j == -1:
                        rows_of(TB * t + m)
                    if fetch and j >= 0:
                        gather(m % 2, j)

            tile(0)
            with pool.Fori(1, NT - 1) as t:
                tile(t)
            tile(NT - 1)

        @block.scalar
        def _(act):
            act.wait_ge(s_angle, 1)
            act.activation(straight[:, 0], reduced[0], ACT.Sin).then_inc(s_trig, 1)
            act.activation(straight[:, 1], reduced[1], ACT.Sin).then_inc(s_trig, 1)
            act.activation(straight[:, 2], reduced[1], ACT.Sin, scale=-1.0).then_inc(s_trig, 1)

            def split_w(j, c, landed):
                act.wait_ge(s_wraw[c], 16 * landed)
                if not isinstance(j, int) or j >= 2:
                    act.wait_ge(s_proj, 2 * NT - 1 if isinstance(j, int) and j == 2 else NT * (j - 1))
                act.activation(w_hi[:, c], w_raw[:, c], ACT.Copy).then_inc(s_whi, 1)

            def high_part(t):
                act.wait_ge(s_x1turn, t + 1)
                act.activation(x1t_hi[:, :, t * P:(t + 1) * P],
                               x1t_ps[:, :].rearrange("p (c n) -> p c n", c=KC), ACT.Copy)\
                   .then_inc(s_x1hi, 1)

            def scale(u, n):
                act.wait_ge(s_rstd, u + 1)
                if after_start(u - 1):
                    act.wait_ge(s_turned, u - 1)
                for g in range(G):
                    last = act.activation(rotated[:, n % 2, g * D:(g + 1) * D],
                                          straight[:, n % 4, g * D:(g + 1) * D], ACT.Copy,
                                          scale=rstd[:, n % 4, g:g + 1])
                last.then_inc(s_scaled, 1)

            def stage(u, n, rounds):
                if after_start(rounds):
                    act.wait_ge(s_stored[n % RING], 16 * rounds)
                act.wait_ge(s_turned, u + 1)
                act.activation(staged[:, n % RING].rearrange("d (b g s) -> d g b s", b=TB, g=G),
                               turn_ps[n % 2][:, :].rearrange("d (g b s) -> d g b s", b=TB, g=G),
                               ACT.Copy).then_inc(s_staged, 1)

            def units(i):
                first, last = isinstance(i, int) and i == 0, isinstance(i, int) and i == QK_BLOCKS // 2
                for n in range(BODY):
                    u = BODY * i + n
                    if first and n == 0:
                        split_w(0, 0, 1)
                    if first and n % 2 == 0:
                        high_part(n // 2)
                    if n == 0 if first else n == 2:
                        split_w(2 * i + 1, 1, i + 1)
                    if (n == BODY - 1 if first else n == NT + 2) and not last:
                        split_w(2 * i + 2, 0, i + 2)
                    if last and n < 4:
                        if n < 2:
                            scale(u - 2, n - 2)
                        for m in ((n,), (n,), (2, 3), ())[n]:
                            stage(BODY * i + m - 4, m - 4, BODY // RING * i + (m - 4) // RING)
                    act.wait_ge(s_proj, u + 1)
                    if last:
                        if n >= 2:
                            act.wait_ge(s_vstored[n % 2], 16 * (n // 2))
                        else:
                            act.wait_ge(s_sumsq, u - 1)
                        act.activation(square[:, n % 2], proj_ps[n % 2][:, :], ACT.Copy)\
                           .then_inc(s_square, 1)
                    else:
                        if after_start(u - 1):
                            act.wait_ge(s_sumsq, u - 1)
                        act.activation(square[:, n % 2], proj_ps[n % 2][:, :], ACT.Square)\
                           .then_inc(s_square, 1)
                    if not (first and n < 2) and not last:
                        scale(u - 2, n - 2)
                    if not (first and n < 4) and not last:
                        stage(u - 4, n - 4, BODY // RING * i + (n - 4) // RING)

            units(0)
            with act.Fori(1, QK_BLOCKS // 2) as i:
                units(i)
            units(QK_BLOCKS // 2)

            def split_k(t, n):
                hk, c, r = n % HK, n // HK % 2, n % 4
                p = TP * t + n
                if hk == 0:
                    act.wait_ge(s_k[c], 16 * K_DMAS * (2 * t + n // HK // 2 + 1))
                if after_start(p - 3):
                    act.wait_ge(s_scores, p - 3)
                act.activation(k_hi[:, r].rearrange("d (a b) -> d a b", b=PSIZE),
                               kt[:, c, :, hk * PSIZE:(hk + 1) * PSIZE], ACT.Copy).then_inc(s_khi, 1)

            def split_q(t, m, h):
                c, cols = m % 2, slice(h * Q_COLS // 2, (h + 1) * Q_COLS // 2)
                if h == 0:
                    act.wait_ge(s_q[c], 16 * (2 * t + m // 2 + 1))
                    if after_start(TB * t + m - 1):
                        act.wait_ge(s_scores, HK * (TB * t + m - 1))
                act.activation(q_hi[:, c, cols], q_raw[:, c, cols], ACT.Copy).then_inc(s_qhi, 1)

            def slot(t, n, do_exp, do_split):
                p = TP * t + n
                if not (isinstance(p, int) and p < 2):
                    act.wait_ge(s_pt, p - 1)
                    if after_start(p - 3):
                        act.wait_ge(s_pv, p - 3)
                    act.activation(probs_t[:, n % 2], pt_ps[n % 2][:, 0:NCH * P], ACT.Copy)\
                       .then_inc(s_ptc, 1)
                if do_split:
                    split_k(t, n + 2)
                if n % HK in Q_SPLITS and not last_sequence(t, n):
                    split_q(t, n // HK + 1, n % HK - Q_SPLITS[0])
                if do_exp:
                    act.wait_ge(s_low, p + 1)
                    act.activation(probs[:, n % 4, 0:KEYS], probs[:, n % 4, 0:KEYS], ACT.Exp,
                                   bias=low[:, n % 4:n % 4 + 1], scale=-1.0,
                                   accum_out=total[:, n % 4:n % 4 + 1]).then_inc(s_exp, 1)

            for h in range(2):
                split_q(0, 0, h)
            split_k(0, 0)
            split_k(0, 1)
            for c in range(2):
                act.wait_ge(s_vstored[c], 16 * (UNITS - QK_UNITS) // 2)
            for n in range(TP):
                slot(0, n, True, True)
            with act.Fori(1, NT - 1) as t:
                for n in range(TP):
                    slot(t, n, True, True)
            for n in range(TP + 2):
                slot(NT - 1, n, n < TP, n < TP - 2)

            def head(i, n):
                c, g, h = n // G, n % G, HEADS * i + n
                if g == 0:
                    act.wait_ge(s_oin[c], 32 * (i + 1))
                if after_start(h - 1):
                    act.wait_ge(s_wo, h - 1)
                act.activation(o_hi[:, n % 2].rearrange("d (b s) -> d b s", s=SEQ),
                               o_raw[c][:, :, g * SEQ:(g + 1) * SEQ], ACT.Copy)
                act.activation(wo_hi[:, n % 2], wo_raw[c][:, g], ACT.Copy).then_inc(s_ohi, 1)

            for n in range(HEADS):
                head(0, n)
            with act.Fori(1, HK // 2) as i:
                for n in range(HEADS):
                    head(i, n)
            for t in range(NT):
                act.wait_ge(s_r3turn, t + 1)
                act.activation(r3t[:, t], acc[t][:, :].rearrange("p (c n) -> p c n", c=KC), ACT.Copy)\
                   .then_inc(s_r3t, 1)
            act.wait_ge(s_gap, 1)
            act.activation(gate[:, 1], gate[:, 0], ACT.Exp).then_inc(s_gexp, 1)

        @block.tensor
        def _(pe):
            pe.wait_ge(s_const, 16 * N_CONST)
            def turn_x1(t):
                pe.wait_ge(s_x1, t + 1)
                if t >= 1:
                    pe.wait_ge(s_x1lo, t)
                for k in range(KC):
                    last = pe.transpose(x1t_ps[:, k * P:(k + 1) * P], x1[:, t % 2, k * P:(k + 1) * P],
                                        ident)
                last.then_inc(s_x1turn, 1)

            def layer_0(t):
                c = t % 2
                pe.wait_ge(s_l0in[c], 16 * (TB + 2) * (t // 2 + 1))
                if t >= 2:
                    pe.wait_ge(s_x1, t - 1)
                for k in range(KC):
                    for b in range(TB):
                        last = pe.matmul(l0_ps[c][SEQ * b:SEQ * b + SEQ, :],
                                         x0t[:, c, k, SEQ * b:SEQ * b + SEQ], w0_sb[:, c, b, k, :],
                                         start=(k == 0), stop=(k == KC - 1))
                last.then_inc(s_l0, 1)
                turn_x1(t)

            def project(i, n):
                t, c = place(i, n)
                for k in range(KC):
                    xs, ws = slice(t * P, (t + 1) * P), slice(k * HID, (k + 1) * HID)
                    for a, w in ((x1t_hi, w_hi), (x1t_hi, w_lo), (x1t_lo, w_hi)):
                        last = pe.matmul(proj_ps[n % 2][:, :], a[:, k, xs], w[:, c, ws],
                                         start=(k == 0 and w is w_hi and a is x1t_hi),
                                         stop=(k == KC - 1 and a is x1t_lo))
                last.then_inc(s_proj, 1)

            def turn(u, n):
                pe.wait_ge(s_scaled, u + 1)
                if after_start(u - 1):
                    pe.wait_ge(s_staged, u - 1)
                for g in range(G):
                    last = pe.transpose(turn_ps[n % 2][:, g * P:(g + 1) * P],
                                        rotated[:, n % 2, g * D:(g + 1) * D], ident)
                last.then_inc(s_turned, 1)

            def units(i):
                first, last = isinstance(i, int) and i == 0, isinstance(i, int) and i == QK_BLOCKS // 2
                for n in range(BODY):
                    u = BODY * i + n
                    if first and n % 2 == 0:
                        layer_0(n // 2)
                        pe.wait_ge(s_x1lo, n // 2 + 1)
                    if n < 2 if first else n % NT == 0:
                        pe.wait_ge(s_wlo, 2 * i + place(i, n)[1] + 1)
                    if after_start(u - 1):
                        if last and n >= 2:
                            pe.wait_ge(s_square, u - 1)
                        else:
                            pe.wait_ge(s_cross, u - 1)
                    project(i, n)
                    if not (first and n < 3) and not (last and n >= 3):
                        turn(u - 3, n - 3)

            units(0)
            with pe.Fori(1, QK_BLOCKS // 2) as i:
                units(i)
            units(QK_BLOCKS // 2)

            def scores(t, n):
                p, hk, c, r = TP * t + n, n % HK, n // HK % 2, n % 4
                if hk == 0:
                    pe.wait_ge(s_qlo, 2 * (TB * t + n // HK + 1))
                pe.wait_ge(s_klo, p + 1)
                if after_start(p):
                    pe.wait_ge(s_low, p)
                for lo, hi in ((0, SPLIT), (SPLIT, KEYS)):
                    for q, k in ((q_hi, k_hi), (q_hi, k_lo), (q_lo, k_hi)):
                        last = pe.matmul(scores_ps[:, lo:hi], q[:, c, hk * P:(hk + 1) * P],
                                         k[:, r, lo:hi], start=(q is q_hi and k is k_hi),
                                         stop=(q is q_lo))
                last.then_inc(s_scores, 1)

            def turn_probs(p, n):
                pe.wait_ge(s_norm, p + 1)
                if after_start(p - 1):
                    pe.wait_ge(s_ptc, p - 1)
                for j in range(NCH):
                    last = pe.transpose(pt_ps[n % 2][:, j * P:(j + 1) * P],
                                        probs[:, n % 4, j * P:(j + 1) * P], ident)
                last.then_inc(s_pt, 1)

            def values(p, n, arrived):
                hk, c = n % HK, n // HK % 2
                if hk == 0:
                    pe.wait_ge(s_v[c], 16 * (NCH - 1) * arrived)
                    pe.wait_ge(s_vnew[c], 16 * arrived)
                pe.wait_ge(s_ptc, p + 1)
                if after_start(p - 1):
                    pe.wait_ge(s_o, p - 1)
                for j in range(NCH):
                    last = pe.matmul(o_ps[n % 2][:, 0:P], vt[:, c, j, hk * D:(hk + 1) * D],
                                     probs_t[:, n % 2, j * P:(j + 1) * P],
                                     start=(j == 0), stop=(j == NCH - 1))
                last.then_inc(s_pv, 1)

            def slot(t, n, do_scores, do_turn, do_values):
                p = TP * t + n
                if do_scores:
                    scores(t, n)
                if do_turn:
                    turn_probs(p - 2, n - 2)
                if do_values:
                    values(p - 3, (n - 3) % TP, 2 * t + (n - 3) // (2 * HK) + 1)

            pe.wait_ge(s_blank, 1)
            for n in range(TP):
                slot(0, n, True, n >= 2, n >= 3)
            with pe.Fori(1, NT) as t:
                for n in range(TP):
                    slot(t, n, True, True, True)
            for n in range(3):
                slot(NT, n, False, n < 2, True)

            def head(i, n, first, last_head):
                pe.wait_ge(s_olo, HEADS * i + n + 1)
                for t in range(NT):
                    for a, w in ((o_hi, wo_hi), (o_hi, wo_lo), (o_lo, wo_hi)):
                        last = pe.matmul(acc[t][:, :], a[:, n % 2, t * P:(t + 1) * P], w[:, n % 2],
                                         start=(first and a is o_hi and w is wo_hi),
                                         stop=(last_head and a is o_lo))
                    if last_head:
                        last.then_inc(s_acc, 1)
                if not last_head:
                    last.then_inc(s_wo, 1)

            pe.wait_ge(s_o, PAIRS)
            pe.wait_ge(s_ptc, PAIRS)
            for n in range(HEADS):
                head(0, n, n == 0, False)
            with pe.Fori(1, HK // 2 - 1) as i:
                for n in range(HEADS):
                    head(i, n, False, False)
            for n in range(HEADS):
                head(HK // 2 - 1, n, False, n == HEADS - 1)

            pe.wait_ge(s_late2, 16 * NB)
            for t in range(NT):
                pe.wait_ge(s_res2, t + 1)
                pe.matmul(acc[t][:, :], w2_sb[:, t], res2[:, t], start=True, stop=True).then_inc(s_l2, 1)
            for t in range(NT):
                pe.wait_ge(s_res3, t + 1)
                for k in range(KC):
                    last = pe.transpose(acc[t][:, k * P:(k + 1) * P], res3[:, t, k * P:(k + 1) * P], ident)
                last.then_inc(s_r3turn, 1)
            pe.wait_ge(s_late, 16 * 4)
            for t in range(NT):
                pe.wait_ge(s_r3t, t + 1)
                for k in range(KC):
                    last = pe.matmul(acc[t][:, 0:ER + E], r3t[:, t, k], a3_sb[:, k], start=(k == 0),
                                     stop=(k == KC - 1))
                last.then_inc(s_hid, 1)

            def base(t):
                for k in range(KC):
                    pe.matmul(acc[t][:, :], r3t[:, t, k], w3_sb[:, k], start=(k == 0), stop=False)

            for t in range(NT - 2):
                pe.wait_ge(s_hidc, t + 1)
                base(t)
            pe.wait_ge(s_hidc, NT)
            pe.wait_ge(s_gated, 1)
            for t in range(NT):
                last = pe.transpose(gated_ps(t), hid[:, t, 0:ER], ident)
            last.then_inc(s_gturn, 1)
            pe.wait_ge(s_gt, 1)
            for t in range(NT):
                if t >= NT - 2:
                    base(t)
                pe.matmul(acc[t][:, :], gated_t[:, t], b3_sb[:, :], start=False, stop=True)\
                  .then_inc(s_l3, 1)

        @block.vector
        def _(dve):
            dve.wait_ge(s_const, 16 * N_CONST)
            dve.tensor_copy(lens_f[:, :], lens_all[:, :])
            dve.drain()
            for g in range(TB):
                q = slice(SEQ * g, SEQ * g + SEQ)
                dve.tensor_scalar(v_rows[q, :], pages_all[q, g::TB], float(PSIZE), token_no[q], ALU.mult,
                                  ALU.add)
                dve.tensor_scalar(pos[q, :], lens_f[q, g::TB], token_no[q], None, ALU.add)
                dve.tensor_copy(lang_f[q, :], lang_all[q, g::TB])
            dve.drain()
            for t in range(NT):
                last = dve.tensor_scalar(lang_bias[:, t], expert_no, lang_f[:, t:t + 1], LANG_BIAS,
                                         ALU.is_equal, ALU.mult)
                dve.tensor_scalar(angle[:, t * D // 2:(t + 1) * D // 2], freq, pos[:, t:t + 1], None,
                                  ALU.mult)
            last.then_inc(s_index, 1)
            for way, (turn, shift) in enumerate(((0.25, np.pi / 2), (0.0, 0.0))):
                dve.drain()
                dve.tensor_scalar(turns, angle, 1.0 / (2 * np.pi), turn, ALU.mult, ALU.add)
                dve.drain()
                dve.tensor_scalar(turns, turns, ROUND, None, ALU.add)
                dve.drain()
                dve.tensor_scalar(turns, turns, -ROUND, None, ALU.add)
                dve.drain()
                dve.scalar_tensor_tensor(out=reduced[way], in0=turns, scalar=-TURN_A, in1=angle,
                                         op0=ALU.mult, op1=ALU.add)
                for part in (TURN_B, TURN_C):
                    dve.drain()
                    dve.scalar_tensor_tensor(out=reduced[way], in0=turns, scalar=-part, in1=reduced[way],
                                             op0=ALU.mult, op1=ALU.add)
                dve.drain()
                dve.tensor_scalar(reduced[way], reduced[way], float(shift), SIN_LIMIT, ALU.add, ALU.min)
                dve.drain()
                last = dve.tensor_scalar(reduced[way], reduced[way], -SIN_LIMIT, None, ALU.max)
            last.then_inc(s_angle, 1)
            dve.wait_ge(s_trig, 3)
            H = D // 2
            for w in range(2):
                for half in range(2):
                    here, other = (qk_w[:, w, x * H:(x + 1) * H].unsqueeze(1).to_broadcast([P, NT, H])
                                   for x in (half, 1 - half))
                    cosine, sine = (straight[:, x].rearrange("p (t f) -> p t f", f=H)
                                    for x in (0, 1 if half else 2))
                    dve.tensor_tensor(table[:, 2 * w, :, half * H:(half + 1) * H], cosine, here, ALU.mult)
                    last = dve.tensor_tensor(table[:, 2 * w + 1, :, half * H:(half + 1) * H], sine, other,
                                             ALU.mult)
            last.then_inc(s_table, 1)
            dve.wait_ge(s_table, 1)

            def split_w(j, c):
                dve.wait_ge(s_whi, j + 1)
                dve.tensor_tensor(w_lo[:, c], w_raw[:, c], w_hi[:, c].bitcast(F32), ALU.subtract)\
                   .then_inc(s_wlo, 1)

            def layer_0(t):
                c = t % 2
                dve.wait_ge(s_l0, t + 1)
                if t >= 2:
                    dve.wait_ge(s_x1out[c], 16 * (t // 2))
                    dve.wait_ge(s_x1turn, t - 1)
                dve.tensor_tensor(x1[:, c], l0_ps[c][:, :], x0[:, c], ALU.add).then_inc(s_x1, 1)
                if t == 0:
                    split_w(0, 0)
                dve.wait_ge(s_x1hi, t + 1)
                xs = slice(t * P, (t + 1) * P)
                dve.tensor_tensor(x1t_lo[:, :, xs], x1t_ps[:, :].rearrange("p (c n) -> p c n", c=KC),
                                  x1t_hi[:, :, xs].bitcast(F32), ALU.subtract).then_inc(s_x1lo, 1)

            def units(i, w):
                for n in range(BODY):
                    first = isinstance(i, int) and i == 0
                    u, t = BODY * i + n, place(i, n)[0]
                    if first and n % 2 == 0:
                        layer_0(n // 2)
                    if n == 0 if first else n == 4:
                        split_w(2 * i + 1, 1)
                    if n == BODY - 1 if first else n == NT + 4:
                        split_w(2 * i + 2, 0)
                    both = proj_ps[n % 2][:, :].rearrange("p (g h f) -> p g h f", g=G, h=2)
                    dve.wait_ge(s_square, u + 1)
                    if after_start(u - 3):
                        dve.wait_ge(s_scaled, u - 3)
                    dve.tensor_tensor(straight[:, n % 4].rearrange("p (g d) -> p g d", g=G),
                                      proj_ps[n % 2][:, :].rearrange("p (g d) -> p g d", g=G),
                                      table[:, 2 * w, t:t + 1, :].to_broadcast([P, G, D]), ALU.mult)
                    if after_start(u - 1):
                        dve.wait_ge(s_rot, u - 1)
                    swapped = crossed[:, n % 2].rearrange("p (g h f) -> p g h f", g=G, h=2)
                    for half in range(2):
                        last = dve.tensor_tensor(
                            swapped[:, :, half, :], both[:, :, 1 - half, :],
                            table[:, 2 * w + 1, t:t + 1, half * H:(half + 1) * H].to_broadcast([P, G, H]),
                            ALU.mult)
                    last.then_inc(s_cross, 1)
                    dve.tensor_reduce(sumsq[:, n % 4], square[:, n % 2].rearrange("p (g d) -> p g d", g=G),
                                      AX_X, ALU.add).then_inc(s_sumsq, 1)

            units(0, 0)
            with dve.Fori(1, Q_BLOCKS // 2) as i:
                units(i, 0)
            units(Q_BLOCKS // 2, 1)
            dve.wait_ge(s_proj, QK_UNITS + 4)
            split_w(QKV_BLOCKS - 1, 1)

            for r in range(RING):
                dve.wait_ge(s_stored[r], 16 * QK_UNITS // RING)
            for c in range(2):
                dve.wait_ge(s_x1out[c], 16 * NT // 2)
            dve.memset(vt[SEQ:2 * SEQ, :, NCH - 1], 0.0)
            dve.memset(vt[2 * SEQ:P, :, NCH - 1], 0.0)
            dve.memset(probs[:, :, KEYS:], 0.0)
            dve.memset(mask[:, :, L:], 0.0)
            dve.drain()
            dve.memset(low[:, :], 0.0).then_inc(s_blank, 1)
            dve.drain()

            def write_mask(b, c):
                dve.tensor_scalar(mask[:, c, 0:L], key_no, lens_f[:, bass.ds(b, 1)], MASKED, ALU.is_ge,
                                  ALU.mult)
                dve.drain()

            def split_k(t, n):
                hk, c, r = n % HK, n // HK % 2, n % 4
                dve.wait_ge(s_khi, TP * t + n + 1)
                dve.tensor_tensor(k_lo[:, r].rearrange("d (a b) -> d a b", b=PSIZE),
                                  kt[:, c, :, hk * PSIZE:(hk + 1) * PSIZE],
                                  k_hi[:, r].bitcast(F32).rearrange("d (a b) -> d a b", b=PSIZE),
                                  ALU.subtract).then_inc(s_klo, 1)

            def split_q(t, m, h):
                c, cols = m % 2, slice(h * Q_COLS // 2, (h + 1) * Q_COLS // 2)
                dve.wait_ge(s_qhi, 2 * (TB * t + m) + h + 1)
                dve.tensor_tensor(q_lo[:, c, cols], q_raw[:, c, cols], q_hi[:, c, cols].bitcast(F32),
                                  ALU.subtract).then_inc(s_qlo, 1)

            def slot(t, n, do_pair, do_inverse, do_split, do_o):
                p = TP * t + n
                if do_inverse:
                    dve.wait_ge(s_exp, p)
                if do_pair:
                    dve.wait_ge(s_scores, p + 1)
                if do_inverse:
                    dve.reciprocal(inverse[:, (n - 1) % 4:(n - 1) % 4 + 1],
                                   total[:, (n - 1) % 4:(n - 1) % 4 + 1]).then_inc(s_inv, 1)
                if do_pair:
                    dve.tensor_tensor_reduce(probs[:, n % 4, 0:KEYS], scores_ps, mask[:, n // HK % 2],
                                             -SCALE, 3e38, ALU.add, ALU.min, low[:, n % 4:n % 4 + 1])\
                       .then_inc(s_low, 1)
                if do_split:
                    split_k(t, n + 2)
                if n % HK in Q_SPLITS and not last_sequence(t, n):
                    split_q(t, n // HK + 1, n % HK - Q_SPLITS[0])
                if n % HK == Q_SPLITS[1] + 1 and not last_sequence(t, n):
                    write_mask(TB * t + n // HK + 1, (n // HK + 1) % 2)
                if do_o:
                    k = (n - 3) % TP
                    b, hk = k // HK, k % HK
                    done = 2 * t + (n - 3) // (2 * HK)
                    dve.wait_ge(s_pv, p - 2)
                    if hk == 0 and after_start(done):
                        dve.wait_ge(s_ostored[b % 2], 16 * done)
                    dve.tensor_copy(o_sb[:, b % 2, hk], o_ps[(n - 3) % 2][:, 0:P]).then_inc(s_o, 1)

            write_mask(0, 0)
            for h in range(2):
                split_q(0, 0, h)
            split_k(0, 0)
            split_k(0, 1)
            for c in range(2):
                dve.wait_ge(s_vstored[c], 16 * (UNITS - QK_UNITS) // 2)
            for n in range(TP):
                slot(0, n, True, n >= 1, True, n >= 3)
            with dve.Fori(1, NT - 1) as t:
                for n in range(TP):
                    slot(t, n, True, True, True, True)
            for n in range(TP + 3):
                slot(NT - 1, n, n < TP, n < TP + 1, n < TP - 2, True)

            dve.memset(w2_sb[:, :], 0.0).then_inc(s_w2blank, 1)

            def head(i, n):
                c, g, h = n // G, n % G, HEADS * i + n
                dve.wait_ge(s_ohi, h + 1)
                dve.tensor_tensor(o_lo[:, n % 2].rearrange("d (b s) -> d b s", s=SEQ),
                                  o_raw[c][:, :, g * SEQ:(g + 1) * SEQ],
                                  o_hi[:, n % 2].bitcast(F32).rearrange("d (b s) -> d b s", s=SEQ),
                                  ALU.subtract)
                dve.tensor_tensor(wo_lo[:, n % 2], wo_raw[c][:, g], wo_hi[:, n % 2].bitcast(F32),
                                  ALU.subtract).then_inc(s_olo, 1)

            for n in range(HEADS):
                head(0, n)
            with dve.Fori(1, HK // 2) as i:
                for n in range(HEADS):
                    head(i, n)
            dve.wait_ge(s_late, 16 * 4)
            for t in range(NT):
                dve.wait_ge(s_acc, t + 1)
                dve.tensor_tensor(res2[:, t], acc[t][:, :], res1[:, t], ALU.add).then_inc(s_res2, 1)
            for t in range(NT):
                dve.wait_ge(s_l2, t + 1)
                dve.tensor_tensor(res3[:, t], acc[t][:, :], res2[:, t], ALU.add).then_inc(s_res3, 1)
            for t in range(NT):
                dve.wait_ge(s_hid, t + 1)
                dve.tensor_copy(hid[:, t], acc[t][:, 0:ER + E]).then_inc(s_hidc, 1)
            dve.drain()
            dve.tensor_tensor(logits[:, :, :], hid[:, :, ER:], lang_bias[:, :, :], ALU.add)
            dve.drain()
            for t in range(NT):
                dve.max(top[:, t], logits[:, t])
            dve.drain()
            dve.tensor_tensor(gate[:, 0], top[:, :, 1], top[:, :, 0], ALU.subtract).then_inc(s_gap, 1)
            for t in range(NT):
                dve.max_index(top_at[:, t], top[:, t], logits[:, t])
            dve.drain()
            dve.tensor_copy(top_f[:, :, :], top_at[:, :, :])
            dve.wait_ge(s_gexp, 1)
            dve.tensor_scalar(gate[:, 2], gate[:, 1], 1.0, None, ALU.add)
            dve.drain()
            dve.reciprocal(gate[:, 3], gate[:, 2])
            for x in range(2):
                dve.tensor_tensor(picks[:, x], expert_no.unsqueeze(1).to_broadcast([P, NT, E]),
                                  top_f[:, :, x:x + 1].to_broadcast([P, NT, E]), ALU.is_equal)
            dve.drain()
            dve.tensor_tensor(gate[:, 4], gate[:, 1], gate[:, 3], ALU.mult)
            dve.drain()
            for x in range(2):
                dve.tensor_tensor(picks[:, x], picks[:, x],
                                  gate[:, 3 + x].unsqueeze(2).to_broadcast([P, NT, E]), ALU.mult)
            dve.drain()
            dve.tensor_tensor(picks[:, 0], picks[:, 0], picks[:, 1], ALU.add)
            dve.drain()
            for t in range(NT):
                hidden = hid[:, t, 0:ER].rearrange("p (e r) -> p e r", e=E)
                last = dve.scalar_tensor_tensor(out=hidden, in0=hidden, scalar=SCALING,
                                                in1=picks[:, 0, t].unsqueeze(2).to_broadcast([P, E, R]),
                                                op0=ALU.mult, op1=ALU.mult)
            last.then_inc(s_gated, 1)
            dve.wait_ge(s_gturn, 1)
            for t in range(0, NT, 4):
                last = dve.tensor_copy(gated_t[:, t:t + 4],
                                       acc[NT - 2 + t // 4][:, :].rearrange("p (t n) -> p t n", n=P))
            last.then_inc(s_gt, 1)
            for t in range(NT):
                dve.wait_ge(s_l3, t + 1)
                dve.tensor_tensor(res1[:, t], acc[t][:, :], res3[:, t], ALU.add).then_inc(s_final, 1)


def kernel(**inputs):
    import concourse.bacc as bacc
    from concourse.bass_utils import run_bass_kernel_spmd

    def arr(name):
        return np.asarray(inputs[name])

    def feature_chunks(w):
        return w.T.reshape(KC, P, -1).transpose(1, 0, 2)

    x = arr("x").reshape(NB * SEQ, HID)
    w0 = arr("L0_cond_weight")
    qkv = np.concatenate([arr("L1_cond_Wq"), arr("L1_cond_Wk"), arr("L1_cond_Wv")])
    consts = np.zeros((P, C_ALL), np.float32)
    consts[:, C_IDENT:C_IDENT + P] = np.eye(P)
    power = (10000.0 ** (np.arange(0, D, 2) / D)).astype(np.float32)
    consts[:, C_FREQ:C_FREQ + D // 2] = np.float32(1.0) / power
    consts[:, C_KEY:C_KEY + L] = np.arange(L)
    consts[:, C_EXPERT:C_EXPERT + E] = np.arange(E)
    consts[:, C_TOKEN] = np.arange(P) % SEQ
    arrays = {
        "x_tok": x,
        "x_feat": feature_chunks(x),
        "adapter": arr("itok_B_0_15").reshape(1, NB),
        "pages": arr("itok_Bx16_0_63").reshape(1, NB * NPP),
        "lens": arr("itok_B_207_1644").reshape(1, NB),
        "subject": arr("itok_B_0_30").reshape(1, NB),
        "language": arr("itok_B_0_7").reshape(1, NB),
        "w0": w0.transpose(0, 2, 1).reshape(-1, KC, P, HID).transpose(0, 2, 1, 3),
        "wqkv": qkv.reshape(QKV_BLOCKS, HID, KC, P).transpose(0, 3, 2, 1).reshape(QKV_BLOCKS, P, KC * HID),
        "wo": arr("L1_cond_Wo").reshape(HID, HQ, D).transpose(2, 1, 0),
        "kcache": arr("L1_cond_k_cache").transpose(0, 3, 2, 1).reshape(PAGES, D, HK * PSIZE),
        "vcache": arr("L1_cond_v_cache").reshape(PAGES * PSIZE, HK * D),
        "q_w": arr("L1_cond_q_norm_w").reshape(1, D),
        "k_w": arr("L1_cond_k_norm_w").reshape(1, D),
        "w2": arr("L2_cond_weights"),
        "w3": feature_chunks(arr("L3_cond_W")),
        "a3": feature_chunks(np.concatenate([arr("L3_cond_A").reshape(ER, HID), arr("L3_cond_Wr")])),
        "b3": arr("L3_cond_B").transpose(0, 2, 1).reshape(ER, HID),
        "consts": consts,
    }
    arrays = {k: np.ascontiguousarray(v) for k, v in arrays.items()}
    nc = bacc.Bacc("TRN2", target_bir_lowering=False, num_devices=1)
    aps = {k: nc.dram_tensor(k, v.shape, mybir.dt.from_np(v.dtype), kind="ExternalInput").ap()
           for k, v in arrays.items()}
    out = nc.dram_tensor("out", (NB * SEQ, HID), F32, kind="ExternalOutput").ap()
    build(nc, out=out, **aps)
    got = run_bass_kernel_spmd(nc, [arrays], core_ids=[0]).results[0]["out"]
    return got.reshape(NB, SEQ, HID)
```

```python
from contextlib import ExitStack

import numpy as np

import concourse.bass as bass
from concourse import mybir

F32 = mybir.dt.float32
F32R = mybir.dt.float32r
I32 = mybir.dt.int32
U32 = mybir.dt.uint32
ALU = mybir.AluOpType
ACT = mybir.ActivationFunctionType
AX_X = mybir.AxisListType.X
SP_ENGINE = mybir.EngineType.SP

P = 128
NB, SEQ, HID = 32, 32, 512
D, HQ, HK = 128, 32, 8
G = HQ // HK
PAGES, PSIZE, NPP = 64, 32, 16
L = NPP * PSIZE
KEYS = L + SEQ
NCH = L // P + 1
TB = P // SEQ
NT = NB // TB
KC = HID // P
QKV_BLOCKS = (HQ + 2 * HK) * D // HID
QK_BLOCKS = (HQ + HK) * D // HID
Q_BLOCKS = HQ * D // HID
GT = NT // 2
BODY = 2 * GT
GROUP_ITERS = QK_BLOCKS // 2
ITERS = 2 * GROUP_ITERS
EARLY = 3
QUARTERS = ((0,), (1, 2), (3,))
STREAM = QK_BLOCKS + QKV_BLOCKS
LAYER_0_AT = (0, 1, 3, 5, 12, 17, 22, 27)
QK_ROW = QK_BLOCKS * P
Q_COLS = Q_BLOCKS * P
SLOTS = NPP + 1
E, R = 8, 16
ER = E * R
SCALE = 1.0 / float(np.sqrt(D))
EPS = 1e-6
RING = 4
LANG_BIAS = 5.0
SCALING = 2.0
MASKED = -1e30

C_IDENT, C_FREQ, C_KEY, C_EXPERT, C_TOKEN = 0, P, P + D // 2, P + D // 2 + L, P + D // 2 + L + E
C_ALL = C_TOKEN + 1

TURN_A = 6.28125
TURN_B = float(np.round((2 * np.pi - TURN_A) * 2.0**21) / 2.0**21)
TURN_C = float(np.float32(2 * np.pi - TURN_A - TURN_B))
ROUND = 1.5 * 2.0**23
SIN_LIMIT = 3.1415925


def after_start(value):
    return not isinstance(value, int) or value > 0


def place(i, n):
    if isinstance(i, int) and i == 0:
        return n // 2, n % 2
    second = not isinstance(i, int) or i >= GROUP_ITERS
    return n % GT + (GT if second else 0), n // GT


def block_of(j):
    return j - QK_BLOCKS if not isinstance(j, int) or j >= QK_BLOCKS else j


def tile_of_layer_0(i, n):
    if isinstance(i, int) and BODY * i + n in LAYER_0_AT:
        return LAYER_0_AT.index(BODY * i + n)
    return None


def build(nc, x_tok, x_feat, adapter, pages, lens, subject, language, w0, wqkv, wo, kcache, vcache,
          q_w, k_w, w2, w3, a3, b3, consts, out):
    qk_dram = nc.dram_tensor("qk_scratch", (NB, D, QK_ROW), F32).ap()
    v_dram = nc.dram_tensor("v_scratch", (NB * SEQ, HK * D), F32).ap()
    o_dram = nc.dram_tensor("o_scratch", (NB, D, HQ * SEQ), F32).ap()
    x1_dram = nc.dram_tensor("x1_scratch", (NB * SEQ, HID), F32).ap()

    ctx = ExitStack()
    stage_a, stage_b, stage_c = ExitStack(), ExitStack(), ExitStack()
    with ctx:
        def sem(name):
            return ctx.enter_context(nc.semaphore(name))

        def keep(name, shape, dt=F32):
            return ctx.enter_context(nc.sbuf_tensor(name, shape, dt))

        const = keep("const", [P, C_ALL])
        ident = const[:, C_IDENT:C_IDENT + P]
        freq = const[:, C_FREQ:C_FREQ + D // 2]
        key_no = const[:, C_KEY:C_KEY + L]
        expert_no = const[:, C_EXPERT:C_EXPERT + E]
        token_no = const[:, C_TOKEN:C_TOKEN + 1]
        adapter_sb = keep("adapter_sb", [1, NB], I32)
        subject_sb = keep("subject_sb", [1, NB], I32)
        pages_all = keep("pages_all", [P, NB * NPP], I32)
        lens_f = keep("lens_f", [P, NB])
        v_now = keep("v_now", [P, 2, NCH - 1], U32)
        minus_half = keep("minus_half", [P, G])
        v_rows = keep("v_rows", [P, NB * (NCH - 1)], U32)
        lang_bias = keep("lang_bias", [P, NT, E])

        def sa(name, shape, dt=F32):
            return stage_a.enter_context(nc.sbuf_tensor(name, shape, dt))

        def pa(name):
            return stage_a.enter_context(nc.psum_tensor(name, [P, HID], F32))

        w0_sb = sa("w0_sb", [P, 2, TB, KC, HID])
        x0t = sa("x0t", [P, 2, KC, P])
        x0 = sa("x0", [P, 2, HID])
        x1 = sa("x1", [P, 2, HID])
        w_raw = sa("w_raw", [P, 2, KC * HID])
        straight = sa("straight", [P, 4, HID])
        crossed = sa("crossed", [P, 2, HID])
        rotated = sa("rotated", [P, 2, HID])
        staged = sa("staged", [P, RING, HID])
        sumsq = sa("sumsq", [P, 4, G])
        meansq = sa("meansq", [P, 4, G])
        rstd = sa("rstd", [P, 4, G])
        qk_w = sa("qk_w", [P, 2, D])
        pos = sa("pos", [P, NT])
        lang_f = sa("lang_f", [P, NT])
        lens_all = sa("lens_all", [P, NB], I32)
        lang_all = sa("lang_all", [P, NB], I32)
        table = sa("table", [P, 4, NT, D])
        square = sa("square", [P, 2, HID])
        x1t_hi = sa("x1t_hi", [P, KC, NT * P], F32R)
        x1t_lo = sa("x1t_lo", [P, KC, NT * P], F32R)
        w_hi = sa("w_hi", [P, 2, KC, HID], F32R)
        w_lo = sa("w_lo", [P, 2, KC, HID], F32R)
        angle, turns = square[:, 0, :], square[:, 1, :]
        reduced = [crossed[:, i, :] for i in range(2)]
        l0_ps = [pa(f"l0_ps{i}") for i in range(2)]
        turn_ps = [pa(f"turn_ps{i}") for i in range(2)]
        x1t_ps, _ = pa("x1t_ps"), pa("unused_ps")
        proj_ps = [pa(f"proj_ps{i}") for i in range(2)]
        stage_a.close()

        def sb(name, shape, dt=F32):
            return stage_b.enter_context(nc.sbuf_tensor(name, shape, dt))

        kt = sb("kt", [P, 2, SLOTS, HK * PSIZE])
        vt = sb("vt", [P, 2, NCH, HK * D])
        q_raw = sb("q_raw", [P, 2, Q_COLS])
        q_hi = sb("q_hi", [P, 2, Q_COLS], F32R)
        q_lo = sb("q_lo", [P, 2, Q_COLS], F32R)
        k_hi = sb("k_hi", [P, 4, KEYS], F32R)
        k_lo = sb("k_lo", [P, 4, KEYS], F32R)
        probs = sb("probs", [P, 4, NCH * P])
        mask = sb("mask", [P, 2, KEYS])
        low = sb("low", [P, 4])
        total = sb("total", [P, 4])
        inverse = sb("inverse", [P, 4])
        probs_t = sb("probs_t", [P, 2, NCH * P])
        o_sb = sb("o_sb", [P, 2, HK, P])
        s_ps = stage_b.enter_context(nc.psum_tensor("s_ps", [P, 2 * HID], F32))
        pt_ps = [stage_b.enter_context(nc.psum_tensor(f"pt_ps{i}", [P, 2 * HID], F32)) for i in range(2)]
        o_ps = [stage_b.enter_context(nc.psum_tensor(f"o_ps{i}", [P, HID], F32)) for i in range(2)]
        stage_b.close()
        SPLIT = (SLOTS + 1) // 2 * PSIZE
        scores_ps = s_ps[:, HID - SPLIT:HID - SPLIT + KEYS]

        def sc(name, shape, dt=F32):
            return stage_c.enter_context(nc.sbuf_tensor(name, shape, dt))

        o_raw = [sc(f"o_raw{i}", [P, NB, P]) for i in range(2)]
        wo_hi = sc("wo_hi", [P, 2, HID], F32R)
        wo_raw0 = sc("wo_raw0", [P, G, HID])
        o_hi = sc("o_hi", [P, 2, NB * SEQ], F32R)
        o_lo = sc("o_lo", [P, 2, NB * SEQ], F32R)
        wo_raw = [wo_raw0, sc("wo_raw1", [P, G, HID])]
        wo_lo = sc("wo_lo", [P, 2, HID], F32R)
        w3_sb = sc("w3_sb", [P, KC, HID])
        a3_sb = sc("a3_sb", [P, KC, ER + E])
        b3_sb = sc("b3_sb", [P, HID])
        w2_sb = sc("w2_sb", [P, NT, P])
        res1 = sc("res1", [P, NT, HID])
        res2 = sc("res2", [P, NT, HID])
        res3 = sc("res3", [P, NT, HID])
        r3t = sc("r3t", [P, NT, KC, P])
        hid = sc("hid", [P, NT, ER + E])
        gated_t = sc("gated_t", [P, NT, P])
        logits = sc("logits", [P, NT, E])
        top = sc("top", [P, NT, 8])
        top_at = sc("top_at", [P, NT, 8], U32)
        gate = sc("gate", [P, 6, NT])
        picks = sc("picks", [P, 2, NT, E])
        top_f = sc("top_f", [P, NT, 8])
        acc = [stage_c.enter_context(nc.psum_tensor(f"acc{i}", [P, HID], F32)) for i in range(NT)]
        stage_c.close()

        def gated_ps(t):
            return acc[NT - 2 + t // 4][:, t % 4 * P:(t % 4 + 1) * P]

        s_adapter = sem("s_adapter")
        s_const = sem("s_const")
        s_l0in = [sem(f"s_l0in{i}") for i in range(2)]
        s_x1out = [sem(f"s_x1out{i}") for i in range(2)]
        s_wraw = [sem(f"s_wraw{i}") for i in range(2)]
        s_stored = [sem(f"s_stored{i}") for i in range(RING)]
        s_meansq = sem("s_meansq")
        s_vstored = [sem(f"s_vstored{i}") for i in range(2)]
        s_qkw = sem("s_qkw")
        s_subject = sem("s_subject")
        s_rows = sem("s_rows")
        s_index = sem("s_index")
        s_table = sem("s_table")
        s_angle = sem("s_angle")
        s_trig = sem("s_trig")
        s_l0 = sem("s_l0")
        s_x1 = sem("s_x1")
        s_x1turn = sem("s_x1turn")
        s_x1hi = sem("s_x1hi")
        s_x1lo = sem("s_x1lo")
        s_whi = sem("s_whi")
        s_wlo = sem("s_wlo")
        s_proj = sem("s_proj")
        s_square = sem("s_square")
        s_cross = sem("s_cross")
        s_sumsq = sem("s_sumsq")
        s_rstd = sem("s_rstd")
        s_rot = sem("s_rot")
        s_scaled = sem("s_scaled")
        s_turned = sem("s_turned")
        s_staged = sem("s_staged")

        s_blank = sem("s_blank")
        s_q = [sem(f"s_q{i}") for i in range(2)]
        s_k = [sem(f"s_k{i}") for i in range(2)]
        s_vnew = [sem(f"s_vnew{i}") for i in range(2)]
        s_v = [sem(f"s_v{i}") for i in range(2)]
        s_khi = sem("s_khi")
        s_klo = sem("s_klo")
        s_qhi = sem("s_qhi")
        s_qlo = sem("s_qlo")
        s_scores = sem("s_scores")
        s_low = sem("s_low")
        s_exp = sem("s_exp")
        s_inv = sem("s_inv")
        s_norm = sem("s_norm")
        s_pt = sem("s_pt")
        s_ptc = sem("s_ptc")
        s_pv = sem("s_pv")
        s_o = sem("s_o")
        s_ostored = [sem(f"s_ostored{i}") for i in range(2)]

        s_late = sem("s_late")
        s_late2 = sem("s_late2")
        s_w2blank = sem("s_w2blank")
        s_oin = [sem(f"s_oin{i}") for i in range(2)]
        s_ohi = sem("s_ohi")
        s_olo = sem("s_olo")
        s_wo = sem("s_wo")
        s_acc = sem("s_acc")
        s_res2 = sem("s_res2")
        s_l2 = sem("s_l2")
        s_res3 = sem("s_res3")
        s_r3turn = sem("s_r3turn")
        s_r3t = sem("s_r3t")
        s_hid = sem("s_hid")
        s_hidc = sem("s_hidc")
        s_gap = sem("s_gap")
        s_gexp = sem("s_gexp")
        s_gated = sem("s_gated")
        s_gturn = sem("s_gturn")
        s_gt = sem("s_gt")
        s_l3 = sem("s_l3")
        s_final = sem("s_final")
        s_out = sem("s_out")

        N_CONST = 4
        QK_UNITS, UNITS = QK_BLOCKS * NT, QKV_BLOCKS * NT
        PAIRS, TP = NB * HK, TB * HK
        K_DMAS = NPP + 1
        Q_SPLITS, K_AHEAD = (3, 4), 3
        HEADS = 2 * G

        def last_sequence(t, n):
            return isinstance(t, int) and TB * t + n // HK + 1 >= NB

        block = ctx.enter_context(nc.Block())

        @block.sync
        def _(sp):
            sp.dma_start(adapter_sb[:, :], adapter).then_inc(s_adapter, 16)

            def load_w(j, c):
                if not isinstance(j, int) or j >= 2:
                    sp.wait_ge(s_wlo, KC * (j - 1))
                sp.dma_start(w_raw[:, c:c + 1], wqkv[bass.ds(block_of(j), 1)].rearrange("o p n -> p o n"))\
                  .then_inc(s_wraw[c], 16)

            def load_pages(b, c, with_new=False):
                _, page = nc.values_load_multi_w_load_instructions(
                    pages_all[0:1, bass.ds(b * NPP, NPP)], engines=[SP_ENGINE], min_val=0,
                    max_val=PAGES - 1)
                if with_new:
                    load_new(b, c)
                for j in range(NPP):
                    sp.dma_start(kt[:, c, j], kcache[bass.ds(page[j], 1)].rearrange("o d n -> (o d) n"))\
                      .then_inc(s_k[c], 16)

            def load_new(b, c):
                qk = qk_dram[bass.ds(b, 1)].rearrange("o d n -> (o d) n")
                sp.dma_start(q_raw[:, c], qk[:, 0:Q_COLS]).then_inc(s_q[c], 16)
                sp.dma_start(kt[:, c, NPP], qk[:, Q_COLS:]).then_inc(s_k[c], 16)

            def store(i, n):
                (t, half), r = place(i, n), n % RING
                sp.wait_ge(s_staged, BODY * i + n + 1)
                dst = qk_dram[TB * t:TB * t + TB, :, bass.ds(block_of(2 * i + half) * P, P)]
                sp.dma_start(dst.rearrange("b d n -> d b n"),
                             staged[:, r].rearrange("d (b n) -> d b n", b=TB))\
                  .then_inc(s_stored[r], 16)

            def load_tile(t, parts=range(TB)):
                c = t % 2
                if parts[0] == 0:
                    if t >= 2:
                        sp.wait_ge(s_l0, t - 1)
                        sp.wait_ge(s_x1, t - 1)
                    sp.dma_start(x0t[:, c], x_feat[:, :, t * P:(t + 1) * P]).then_inc(s_l0in[c], 16)
                    sp.dma_start(x0[:, c], x_tok[t * P:(t + 1) * P, :]).then_inc(s_l0in[c], 16)
                if t == 0:
                    sp.wait_ge(s_adapter, 16)
                for b in parts:
                    a = sp.value_load(adapter_sb[0:1, TB * t + b:TB * t + b + 1], min_val=0,
                                      max_val=w0.shape[0] - 1)
                    sp.dma_start(w0_sb[:, c, b], w0[bass.ds(a, 1)].rearrange("o p c n -> (o p) c n"))\
                      .then_inc(s_l0in[c], 16)

            def store_x1(t):
                sp.wait_ge(s_x1, t + 1)
                sp.dma_start(x1_dram[t * P:(t + 1) * P, :], x1[:, t % 2]).then_inc(s_x1out[t % 2], 16)

            load_tile(0)
            load_w(0, 0)
            load_w(1, 1)
            load_tile(1)
            for t in range(EARLY):
                load_tile(t + 2)
                if t == 1:
                    load_w(2, 0)
                    load_w(3, 1)
                store_x1(t)

            def units(i):
                for n in range(BODY):
                    for t in range(EARLY, NT) if isinstance(i, int) else ():
                        part = BODY * i + n - (LAYER_0_AT[t] - RING)
                        if part == 0:
                            store_x1(t)
                        if 0 <= part < TB and t + 2 < NT:
                            load_tile(t + 2, (part,))
                    first, last = (isinstance(i, int) and i == x for x in (0, ITERS - 1))
                    if n == 0 and not first:
                        load_w(2 * i + 3, 1)
                    if (n == 4 if first else n == 2) and not last:
                        load_w(2 * i + 4, 0)
                    store(i, n)
                    if isinstance(i, int) and i == GROUP_ITERS - 1 and n % GT == 2:
                        load_pages(n // GT, n // GT)

            for i in range(GROUP_ITERS):
                units(i)
            with sp.Fori(GROUP_ITERS, ITERS - 1) as i:
                units(i)
            units(ITERS - 1)

            def load_new_v(b, c):
                sp.dma_start(vt[0:SEQ, c, NCH - 1], v_dram[bass.ds(b * SEQ, SEQ), :]).then_inc(s_vnew[c], 16)

            for u in range(QK_UNITS, UNITS):
                t, h, c = u % NT, u // NT - QK_BLOCKS, u % 2
                sp.wait_ge(s_square, u + 1)
                sp.dma_start(v_dram[t * P:(t + 1) * P, h * HID:(h + 1) * HID], square[:, c])\
                  .then_inc(s_vstored[c], 16)
                if u == QK_UNITS + 4:
                    for r in range(RING):
                        sp.wait_ge(s_stored[r], 16 * QK_UNITS // RING)
                    sp.wait_ge(s_wlo, KC * STREAM)
                    load_new(0, 0)
                    load_new(1, 1)
            for c in range(2):
                sp.wait_ge(s_vstored[c], 16 * (UNITS - QK_UNITS) // 2)
            load_new_v(0, 0)
            load_new_v(1, 1)

            def store_o(b, c):
                sp.wait_ge(s_o, HK * (b + 1))
                sp.dma_start(o_dram[bass.ds(b, 1)].rearrange("o d n -> (o d) n"),
                             o_sb[:, c].rearrange("d k n -> d (k n)")).then_inc(s_ostored[c], 16)

            def tile(t):
                for m in range(TB):
                    b, c = TB * t + m, m % 2
                    if isinstance(t, int) and b < 2:
                        continue
                    sp.wait_ge(s_klo, HK * (b - 1))
                    load_pages(b, c, with_new=True)
                    store_o(b - 2, c)
                    sp.wait_ge(s_pv, HK * (b - 1))
                    load_new_v(b, c)

            tile(0)
            with sp.Fori(1, NT) as t:
                tile(t)

            def load_wo(k, c):
                sp.dma_start(wo_raw[c][:, :, :], wo[:, bass.ds(k * G, G), :]).then_inc(s_oin[c], 16)

            def load_heads(k, c, bs=slice(0, NB)):
                sp.dma_start(o_raw[c][:, bs], o_dram[bs, :, bass.ds(k * P, P)].rearrange("b d n -> d b n"))\
                  .then_inc(s_oin[c], 16)

            sp.wait_ge(s_klo, HK * (NB - 1))
            for c in range(2):
                sp.wait_ge(s_ostored[c], 16 * (NB // 2 - 1))
            load_heads(0, 0, slice(0, NB - 2))
            store_o(NB - 2, 0)
            sp.wait_ge(s_pv, HK * (NB - 1))
            load_wo(0, 0)
            for ks in (slice(0, 1), slice(1, HK)):
                sp.wait_ge(s_o, HK * (NB - 1) + ks.stop)
                sp.dma_start(o_dram[NB - 1, :, ks.start * P:ks.stop * P],
                             o_sb[:, 1, ks].rearrange("d k n -> d (k n)")).then_inc(s_ostored[1], 16)
                if ks.start == 0:
                    for c in range(2):
                        sp.wait_ge(s_ostored[c], 16 * NB // 2)
                    load_heads(0, 0, slice(NB - 2, NB))
            sp.wait_ge(s_ostored[1], 16 * (NB // 2 + 1))
            load_wo(1, 1)
            load_heads(1, 1)
            sp.dma_start(w3_sb[:, :, :], w3).then_inc(s_late, 16)
            sp.dma_start(a3_sb[:, :, :], a3).then_inc(s_late, 16)
            sp.dma_start(b3_sb[:, :], b3).then_inc(s_late, 16)
            for c in range(2):
                sp.wait_ge(s_x1out[c], 16 * NT // 2)
            sp.dma_start(res1[:, :, :], x1_dram.rearrange("(t p) n -> p t n", p=P)).then_inc(s_late, 16)
            sp.wait_ge(s_subject, 16)
            sp.wait_ge(s_w2blank, 1)
            for t in range(NT):
                _, subj = nc.values_load_multi_w_load_instructions(
                    subject_sb[0:1, t * TB:(t + 1) * TB], engines=[SP_ENGINE], min_val=0,
                    max_val=w2.shape[0] - 1)
                for b in range(TB):
                    q = slice(SEQ * b, SEQ * b + SEQ)
                    sp.dma_start(w2_sb[q, t, q], w2[bass.ds(subj[b], 1)].rearrange("o c d -> (o c) d"))\
                      .then_inc(s_late2, 16)
            with sp.Fori(1, HK // 2) as i:
                for c in range(2):
                    sp.wait_ge(s_olo, HEADS * (i - 1) + G * (c + 1))
                    load_wo(2 * i + c, c)
                    load_heads(2 * i + c, c)
            for t in range(NT):
                sp.wait_ge(s_final, t + 1)
                sp.dma_start(out[t * P:(t + 1) * P, :], res1[:, t]).then_inc(s_out, 16)
            sp.wait_ge(s_out, 16 * NT)

        @block.gpsimd
        def _(pool):
            pool.memset(minus_half[:, :], -0.5)

            def rows_of(b, c):
                pool.tensor_copy(v_now[:, c], v_rows[:, bass.ds(b * (NCH - 1), NCH - 1)])\
                    .then_inc(s_rows, 1)

            def gather(c, j):
                pool.indirect_dma_start(vt[:, c, j], None, vcache,
                                        bass.IndirectOffsetOnAxis(ap=v_now[:, c, j:j + 1], axis=0))\
                    .then_inc(s_v[c], 16)

            def units(i):
                for n in range(BODY):
                    u, c, r = BODY * i + n, n % 2, n % 4
                    pool.wait_ge(s_cross, u + 1)
                    pool.wait_ge(s_sumsq, u + 1)
                    pool.tensor_tensor(straight[:, r], straight[:, r], crossed[:, c], ALU.add)\
                        .then_inc(s_rot, 1)
                    pool.tensor_scalar(meansq[:, r], sumsq[:, r], 1.0 / D, EPS, ALU.mult, ALU.add)\
                        .then_inc(s_meansq, 1)
                    pool.wait_ge(s_meansq, u + 1)
                    pool.tensor_tensor(rstd[:, r], meansq[:, r], minus_half[:, :], ALU.pow)\
                        .then_inc(s_rstd, 1)
                    if isinstance(i, int) and n % 2 == 0:
                        b, j = i - (GROUP_ITERS - 1), n // 2
                        if j == 0:
                            rows_of(b, b)
                            pool.wait_ge(s_rows, b + 1)
                        gather(b, j)

            with pool.Fori(0, GROUP_ITERS - 1) as i:
                units(i)
            pool.wait_ge(s_index, 1)
            pool.wait_ge(s_x1lo, NT)
            for c in range(2):
                pool.wait_ge(s_x1out[c], 16 * NT // 2)
            units(GROUP_ITERS - 1)
            units(GROUP_ITERS)
            with pool.Fori(GROUP_ITERS + 1, ITERS) as i:
                units(i)

            def tile(t):
                for n in range(TP):
                    p, r = TP * t + n, n % 4
                    m = n // HK + 1
                    j = n % HK - (HK - NCH + 1)
                    fetch = not (isinstance(t, int) and TB * t + m in (1, NB))
                    if fetch and j == -1:
                        pool.wait_ge(s_v[m % 2], 16 * (NCH - 1) * (2 * t + m // 2))
                    if fetch and j == 0:
                        pool.wait_ge(s_rows, TB * t + m + 1)
                        pool.wait_ge(s_pv, HK * (TB * t + m - 1))
                    pool.wait_ge(s_inv, p + 1)
                    pool.tensor_tensor(probs[:, r, 0:KEYS], probs[:, r, 0:KEYS],
                                       inverse[:, r:r + 1].to_broadcast([P, KEYS]), ALU.mult)\
                        .then_inc(s_norm, 1)
                    if fetch and j == -1:
                        rows_of(TB * t + m, m % 2)
                    if fetch and j >= 0:
                        gather(m % 2, j)

            tile(0)
            with pool.Fori(1, NT - 1) as t:
                tile(t)
            tile(NT - 1)

        @block.scalar
        def _(act):
            for dst, src in ((lens_all[:, :], lens.partition_broadcast(P)), (const[:, :], consts),
                             (pages_all[:, :], pages.partition_broadcast(P)),
                             (lang_all[:, :], language.partition_broadcast(P))):
                act.dma_start(dst, src).then_inc(s_const, 16)
            for w, src in enumerate((q_w, k_w)):
                act.dma_start(qk_w[:, w, :], src.partition_broadcast(P)).then_inc(s_qkw, 16)
            act.dma_start(subject_sb[:, :], subject).then_inc(s_subject, 16)
            act.wait_ge(s_angle, 1)
            act.activation(straight[:, 0], reduced[0], ACT.Sin).then_inc(s_trig, 1)
            act.activation(straight[:, 1], reduced[1], ACT.Sin).then_inc(s_trig, 1)
            act.activation(straight[:, 2], reduced[1], ACT.Sin, scale=-1.0).then_inc(s_trig, 1)

            def split_w(j, c, landed, quarters=range(KC)):
                if quarters[0] == 0:
                    act.wait_ge(s_wraw[c], 16 * landed)
                    if not isinstance(j, int) or j >= 2:
                        act.wait_ge(s_proj, BODY - 1 if isinstance(j, int) and j == 2 else GT * (j - 1))
                for k in quarters:
                    act.activation(w_hi[:, c, k], w_raw[:, c, k * HID:(k + 1) * HID], ACT.Copy)\
                       .then_inc(s_whi, 1)

            def high_part(t):
                act.wait_ge(s_x1turn, t + 1)
                act.activation(x1t_hi[:, :, t * P:(t + 1) * P],
                               x1t_ps[:, :].rearrange("p (c n) -> p c n", c=KC), ACT.Copy)\
                   .then_inc(s_x1hi, 1)

            def scale(u, n):
                act.wait_ge(s_rstd, u + 1)
                if after_start(u - 1):
                    act.wait_ge(s_turned, u - 1)
                for g in range(G):
                    last = act.activation(rotated[:, n % 2, g * D:(g + 1) * D],
                                          straight[:, n % 4, g * D:(g + 1) * D], ACT.Copy,
                                          scale=rstd[:, n % 4, g:g + 1])
                last.then_inc(s_scaled, 1)

            def stage(u, n, rounds):
                if after_start(rounds):
                    act.wait_ge(s_stored[n % RING], 16 * rounds)
                act.wait_ge(s_turned, u + 1)
                act.activation(staged[:, n % RING].rearrange("d (b g s) -> d g b s", b=TB, g=G),
                               turn_ps[n % 2][:, :].rearrange("d (g b s) -> d g b s", b=TB, g=G),
                               ACT.Copy).then_inc(s_staged, 1)

            def units(i):
                first = isinstance(i, int) and i == 0
                for n in range(BODY):
                    u, t = BODY * i + n, tile_of_layer_0(i, n)
                    if first and n == 0:
                        split_w(0, 0, 1)
                    if t == 0:
                        high_part(t)
                    if first and n == 0:
                        split_w(1, 1, 1)
                    if first and n == BODY - 1:
                        split_w(2, 0, 2)
                    if not first and n % GT < len(QUARTERS):
                        split_w(2 * i + 1 + n // GT, 1 - n // GT, i + 1 + n // GT, QUARTERS[n % GT])
                    act.wait_ge(s_proj, u + 1)
                    if after_start(u - 1):
                        act.wait_ge(s_sumsq, u - 1)
                    act.activation(square[:, n % 2], proj_ps[n % 2][:, :], ACT.Square)\
                       .then_inc(s_square, 1)
                    if not (first and n < 2):
                        scale(u - 2, n - 2)
                    if not (first and n < RING):
                        stage(u - RING, n - RING, BODY // RING * i + (n - RING) // RING)
                    if t is not None and t > 0:
                        high_part(t)

            for i in range(GROUP_ITERS):
                units(i)
            with act.Fori(GROUP_ITERS, ITERS) as i:
                units(i)
            def split_k(t, n):
                hk, c, r = n % HK, n // HK % 2, n % 4
                p = TP * t + n
                if hk == 0:
                    act.wait_ge(s_k[c], 16 * K_DMAS * (2 * t + n // HK // 2 + 1))
                if after_start(p - 3):
                    act.wait_ge(s_scores, p - 3)
                act.activation(k_hi[:, r].rearrange("d (a b) -> d a b", b=PSIZE),
                               kt[:, c, :, hk * PSIZE:(hk + 1) * PSIZE], ACT.Copy).then_inc(s_khi, 1)

            def split_q(t, m, h):
                c, cols = m % 2, slice(h * Q_COLS // 2, (h + 1) * Q_COLS // 2)
                if h == 0:
                    act.wait_ge(s_q[c], 16 * (2 * t + m // 2 + 1))
                    if after_start(TB * t + m - 1):
                        act.wait_ge(s_scores, HK * (TB * t + m - 1))
                act.activation(q_hi[:, c, cols], q_raw[:, c, cols], ACT.Copy).then_inc(s_qhi, 1)

            for n in range(UNITS - QK_UNITS):
                u = QK_UNITS + n
                if n == UNITS - QK_UNITS - 5:
                    for h in range(2):
                        split_q(0, 0, h)
                if n == UNITS - QK_UNITS - 4:
                    for m in range(K_AHEAD):
                        split_k(0, m)
                if n == 2:
                    split_w(STREAM - 1, 1, STREAM // 2)
                if n < 2:
                    scale(u - 2, n - 2)
                for m in ((0,), (1,), (2, 3))[n] if n < 3 else ():
                    stage(QK_UNITS + m - RING, m - RING, (QK_UNITS + m - RING) // RING)
                act.wait_ge(s_proj, u + 1)
                if n >= 2:
                    act.wait_ge(s_vstored[n % 2], 16 * (n // 2))
                else:
                    act.wait_ge(s_sumsq, u - 1)
                act.activation(square[:, n % 2], proj_ps[n % 2][:, :], ACT.Copy).then_inc(s_square, 1)

            def slot(t, n, do_exp, do_split):
                p = TP * t + n
                if isinstance(p, int) and p == 2:
                    for c in range(2):
                        act.wait_ge(s_vstored[c], 16 * (UNITS - QK_UNITS) // 2)
                if not (isinstance(p, int) and p < 2):
                    act.wait_ge(s_pt, p - 1)
                    if after_start(p - 3):
                        act.wait_ge(s_pv, p - 3)
                    act.activation(probs_t[:, n % 2], pt_ps[n % 2][:, 0:NCH * P], ACT.Copy)\
                       .then_inc(s_ptc, 1)
                if do_split:
                    split_k(t, n + K_AHEAD)
                if n % HK in Q_SPLITS and not last_sequence(t, n):
                    split_q(t, n // HK + 1, n % HK - Q_SPLITS[0])
                if do_exp:
                    act.wait_ge(s_low, p + 1)
                    act.activation(probs[:, n % 4, 0:KEYS], probs[:, n % 4, 0:KEYS], ACT.Exp,
                                   bias=low[:, n % 4:n % 4 + 1], scale=-1.0,
                                   accum_out=total[:, n % 4:n % 4 + 1]).then_inc(s_exp, 1)

            for n in range(TP):
                slot(0, n, True, True)
            with act.Fori(1, NT - 1) as t:
                for n in range(TP):
                    slot(t, n, True, True)
            for n in range(TP + 2):
                slot(NT - 1, n, n < TP, n < TP - K_AHEAD)

            def head(i, n):
                c, g, h = n // G, n % G, HEADS * i + n
                if g == 0:
                    act.wait_ge(s_oin[c], 32 * (i + 1) + (16 if c == 0 else 0))
                if after_start(h - 1):
                    act.wait_ge(s_wo, h - 1)
                act.activation(o_hi[:, n % 2].rearrange("d (b s) -> d b s", s=SEQ),
                               o_raw[c][:, :, g * SEQ:(g + 1) * SEQ], ACT.Copy)
                act.activation(wo_hi[:, n % 2], wo_raw[c][:, g], ACT.Copy).then_inc(s_ohi, 1)

            for n in range(HEADS):
                head(0, n)
            with act.Fori(1, HK // 2) as i:
                for n in range(HEADS):
                    head(i, n)
            for t in range(NT):
                act.wait_ge(s_r3turn, t + 1)
                act.activation(r3t[:, t], acc[t][:, :].rearrange("p (c n) -> p c n", c=KC), ACT.Copy)\
                   .then_inc(s_r3t, 1)
            act.wait_ge(s_gap, 1)
            act.activation(gate[:, 1], gate[:, 0], ACT.Exp).then_inc(s_gexp, 1)

        @block.tensor
        def _(pe):
            pe.wait_ge(s_const, 16 * N_CONST)
            def turn_x1(t):
                pe.wait_ge(s_x1, t + 1)
                if t >= 1:
                    pe.wait_ge(s_x1lo, t)
                for k in range(KC):
                    last = pe.transpose(x1t_ps[:, k * P:(k + 1) * P], x1[:, t % 2, k * P:(k + 1) * P],
                                        ident)
                last.then_inc(s_x1turn, 1)

            def layer_0(t):
                c = t % 2
                pe.wait_ge(s_l0in[c], 16 * (TB + 2) * (t // 2 + 1))
                if t >= 2:
                    pe.wait_ge(s_x1, t - 1)
                for k in range(KC):
                    for b in range(TB):
                        last = pe.matmul(l0_ps[c][SEQ * b:SEQ * b + SEQ, :],
                                         x0t[:, c, k, SEQ * b:SEQ * b + SEQ], w0_sb[:, c, b, k, :],
                                         start=(k == 0), stop=(k == KC - 1))
                last.then_inc(s_l0, 1)

            def project(n, t, c, j):
                xs = slice(t * P, (t + 1) * P)
                for k in range(KC):
                    if j is not None:
                        pe.wait_ge(s_wlo, KC * j + k + 1)
                    for a, w in ((x1t_hi, w_hi), (x1t_hi, w_lo), (x1t_lo, w_hi)):
                        last = pe.matmul(proj_ps[n % 2][:, :], a[:, k, xs], w[:, c, k],
                                         start=(k == 0 and w is w_hi and a is x1t_hi),
                                         stop=(k == KC - 1 and a is x1t_lo))
                last.then_inc(s_proj, 1)

            def turn(u, n):
                pe.wait_ge(s_scaled, u + 1)
                if after_start(u - 1):
                    pe.wait_ge(s_staged, u - 1)
                for g in range(G):
                    last = pe.transpose(turn_ps[n % 2][:, g * P:(g + 1) * P],
                                        rotated[:, n % 2, g * D:(g + 1) * D], ident)
                last.then_inc(s_turned, 1)

            def units(i):
                first = isinstance(i, int) and i == 0
                for n in range(BODY):
                    u, t = BODY * i + n, tile_of_layer_0(i, n)
                    if t is not None:
                        layer_0(t)
                    if t == 0:
                        turn_x1(t)
                    if first and n % 2 == 0:
                        pe.wait_ge(s_x1lo, n // 2 + 1)
                    if after_start(u - 1):
                        pe.wait_ge(s_cross, u - 1)
                    t_of_unit, half = place(i, n)
                    new_block = n < 2 if first else n % GT == 0
                    project(n, t_of_unit, half, 2 * i + half if new_block else None)
                    if t is not None and t > 0:
                        turn_x1(t)
                    if not (first and n < 3):
                        turn(u - 3, n - 3)

            for i in range(GROUP_ITERS):
                units(i)
            pe.wait_ge(s_x1lo, NT)
            with pe.Fori(GROUP_ITERS, ITERS) as i:
                units(i)
            for n in range(UNITS - QK_UNITS):
                u = QK_UNITS + n
                if n < 2:
                    pe.wait_ge(s_cross, u - 1)
                else:
                    pe.wait_ge(s_square, u - 1)
                project(n, n % NT, n // NT, 2 * ITERS + n // NT if n % NT == 0 else None)
                if n < 3:
                    turn(u - 3, n - 3)

            def scores(t, n):
                p, hk, c, r = TP * t + n, n % HK, n // HK % 2, n % 4
                if hk == 0:
                    pe.wait_ge(s_qlo, 2 * (TB * t + n // HK + 1))
                pe.wait_ge(s_klo, p + 1)
                if after_start(p):
                    pe.wait_ge(s_low, p)
                for lo, hi in ((0, SPLIT), (SPLIT, KEYS)):
                    for q, k in ((q_hi, k_hi), (q_hi, k_lo), (q_lo, k_hi)):
                        last = pe.matmul(scores_ps[:, lo:hi], q[:, c, hk * P:(hk + 1) * P],
                                         k[:, r, lo:hi], start=(q is q_hi and k is k_hi),
                                         stop=(q is q_lo))
                last.then_inc(s_scores, 1)

            def turn_probs(p, n):
                pe.wait_ge(s_norm, p + 1)
                if after_start(p - 1):
                    pe.wait_ge(s_ptc, p - 1)
                for j in range(NCH):
                    last = pe.transpose(pt_ps[n % 2][:, j * P:(j + 1) * P],
                                        probs[:, n % 4, j * P:(j + 1) * P], ident)
                last.then_inc(s_pt, 1)

            def values(p, n, arrived):
                hk, c = n % HK, n // HK % 2
                if hk == 0:
                    pe.wait_ge(s_v[c], 16 * (NCH - 1) * arrived)
                    pe.wait_ge(s_vnew[c], 16 * arrived)
                pe.wait_ge(s_ptc, p + 1)
                if after_start(p - 1):
                    pe.wait_ge(s_o, p - 1)
                for j in range(NCH):
                    last = pe.matmul(o_ps[n % 2][:, 0:P], vt[:, c, j, hk * D:(hk + 1) * D],
                                     probs_t[:, n % 2, j * P:(j + 1) * P],
                                     start=(j == 0), stop=(j == NCH - 1))
                last.then_inc(s_pv, 1)

            def slot(t, n, do_scores, do_turn, do_values):
                p = TP * t + n
                if do_scores:
                    scores(t, n)
                if do_turn:
                    turn_probs(p - 2, n - 2)
                if do_values:
                    values(p - 3, (n - 3) % TP, 2 * t + (n - 3) // (2 * HK) + 1)

            pe.wait_ge(s_blank, 1)
            for n in range(TP):
                slot(0, n, True, n >= 2, n >= 3)
            with pe.Fori(1, NT) as t:
                for n in range(TP):
                    slot(t, n, True, True, True)
            for n in range(3):
                slot(NT, n, False, n < 2, True)

            def head(i, n, first, last_head):
                pe.wait_ge(s_olo, HEADS * i + n + 1)
                for t in range(NT):
                    for a, w in ((o_hi, wo_hi), (o_hi, wo_lo), (o_lo, wo_hi)):
                        last = pe.matmul(acc[t][:, :], a[:, n % 2, t * P:(t + 1) * P], w[:, n % 2],
                                         start=(first and a is o_hi and w is wo_hi),
                                         stop=(last_head and a is o_lo))
                    if last_head:
                        last.then_inc(s_acc, 1)
                if not last_head:
                    last.then_inc(s_wo, 1)

            pe.wait_ge(s_o, PAIRS)
            pe.wait_ge(s_ptc, PAIRS)
            for n in range(HEADS):
                head(0, n, n == 0, False)
            with pe.Fori(1, HK // 2 - 1) as i:
                for n in range(HEADS):
                    head(i, n, False, False)
            for n in range(HEADS):
                head(HK // 2 - 1, n, False, n == HEADS - 1)

            pe.wait_ge(s_late2, 16 * NB)
            for t in range(NT):
                pe.wait_ge(s_res2, t + 1)
                pe.matmul(acc[t][:, :], w2_sb[:, t], res2[:, t], start=True, stop=True).then_inc(s_l2, 1)
            for t in range(NT):
                pe.wait_ge(s_res3, t + 1)
                for k in range(KC):
                    last = pe.transpose(acc[t][:, k * P:(k + 1) * P], res3[:, t, k * P:(k + 1) * P], ident)
                last.then_inc(s_r3turn, 1)
            pe.wait_ge(s_late, 16 * 4)
            for t in range(NT):
                pe.wait_ge(s_r3t, t + 1)
                for k in range(KC):
                    last = pe.matmul(acc[t][:, 0:ER + E], r3t[:, t, k], a3_sb[:, k], start=(k == 0),
                                     stop=(k == KC - 1))
                last.then_inc(s_hid, 1)

            def base(t):
                for k in range(KC):
                    pe.matmul(acc[t][:, :], r3t[:, t, k], w3_sb[:, k], start=(k == 0), stop=False)

            for t in range(NT - 2):
                pe.wait_ge(s_hidc, t + 1)
                base(t)
            pe.wait_ge(s_hidc, NT)
            pe.wait_ge(s_gated, 1)
            for t in range(NT):
                last = pe.transpose(gated_ps(t), hid[:, t, 0:ER], ident)
            last.then_inc(s_gturn, 1)
            pe.wait_ge(s_gt, 1)
            for t in range(NT):
                if t >= NT - 2:
                    base(t)
                pe.matmul(acc[t][:, :], gated_t[:, t], b3_sb[:, :], start=False, stop=True)\
                  .then_inc(s_l3, 1)

        @block.vector
        def _(dve):
            dve.wait_ge(s_const, 16 * N_CONST)
            dve.tensor_copy(lens_f[:, :], lens_all[:, :])
            dve.drain()
            for g in range(TB):
                q = slice(SEQ * g, SEQ * g + SEQ)
                dve.tensor_scalar(v_rows[q, :], pages_all[q, g::TB], float(PSIZE), token_no[q], ALU.mult,
                                  ALU.add)
                dve.tensor_scalar(pos[q, :], lens_f[q, g::TB], token_no[q], None, ALU.add)
                dve.tensor_copy(lang_f[q, :], lang_all[q, g::TB])
            dve.drain()
            for t in range(NT):
                last = dve.tensor_scalar(lang_bias[:, t], expert_no, lang_f[:, t:t + 1], LANG_BIAS,
                                         ALU.is_equal, ALU.mult)
                dve.tensor_scalar(angle[:, t * D // 2:(t + 1) * D // 2], freq, pos[:, t:t + 1], None,
                                  ALU.mult)
            last.then_inc(s_index, 1)
            for way, (turn, shift) in enumerate(((0.25, np.pi / 2), (0.0, 0.0))):
                dve.drain()
                dve.tensor_scalar(turns, angle, 1.0 / (2 * np.pi), turn, ALU.mult, ALU.add)
                dve.drain()
                dve.tensor_scalar(turns, turns, ROUND, None, ALU.add)
                dve.drain()
                dve.tensor_scalar(turns, turns, -ROUND, None, ALU.add)
                dve.drain()
                dve.scalar_tensor_tensor(out=reduced[way], in0=turns, scalar=-TURN_A, in1=angle,
                                         op0=ALU.mult, op1=ALU.add)
                for part in (TURN_B, TURN_C):
                    dve.drain()
                    dve.scalar_tensor_tensor(out=reduced[way], in0=turns, scalar=-part, in1=reduced[way],
                                             op0=ALU.mult, op1=ALU.add)
                dve.drain()
                dve.tensor_scalar(reduced[way], reduced[way], float(shift), SIN_LIMIT, ALU.add, ALU.min)
                dve.drain()
                last = dve.tensor_scalar(reduced[way], reduced[way], -SIN_LIMIT, None, ALU.max)
            last.then_inc(s_angle, 1)
            dve.wait_ge(s_trig, 3)
            dve.wait_ge(s_qkw, 32)
            H = D // 2
            for w in range(2):
                for half in range(2):
                    here, other = (qk_w[:, w, x * H:(x + 1) * H].unsqueeze(1).to_broadcast([P, NT, H])
                                   for x in (half, 1 - half))
                    cosine, sine = (straight[:, x].rearrange("p (t f) -> p t f", f=H)
                                    for x in (0, 1 if half else 2))
                    dve.tensor_tensor(table[:, 2 * w, :, half * H:(half + 1) * H], cosine, here, ALU.mult)
                    last = dve.tensor_tensor(table[:, 2 * w + 1, :, half * H:(half + 1) * H], sine, other,
                                             ALU.mult)
            last.then_inc(s_table, 1)
            dve.wait_ge(s_table, 1)

            def split_w(j, c, quarters=range(KC)):
                for k in quarters:
                    dve.wait_ge(s_whi, KC * j + k + 1)
                    dve.tensor_tensor(w_lo[:, c, k], w_raw[:, c, k * HID:(k + 1) * HID],
                                      w_hi[:, c, k].bitcast(F32), ALU.subtract).then_inc(s_wlo, 1)

            def layer_0_sum(t):
                c = t % 2
                dve.wait_ge(s_l0, t + 1)
                if t >= 2:
                    dve.wait_ge(s_x1out[c], 16 * (t // 2))
                    dve.wait_ge(s_x1turn, t - 1)
                dve.tensor_tensor(x1[:, c], l0_ps[c][:, :], x0[:, c], ALU.add).then_inc(s_x1, 1)

            def low_part(t):
                dve.wait_ge(s_x1hi, t + 1)
                xs = slice(t * P, (t + 1) * P)
                dve.tensor_tensor(x1t_lo[:, :, xs], x1t_ps[:, :].rearrange("p (c n) -> p c n", c=KC),
                                  x1t_hi[:, :, xs].bitcast(F32), ALU.subtract).then_inc(s_x1lo, 1)

            def units(i, w):
                for n in range(BODY):
                    first = isinstance(i, int) and i == 0
                    u, t, new = BODY * i + n, place(i, n)[0], tile_of_layer_0(i, n)
                    if new is not None:
                        layer_0_sum(new)
                    if first and n == 0:
                        split_w(0, 0)
                    if new == 0:
                        low_part(new)
                    if first and n == 0:
                        split_w(1, 1)
                    if first and n == BODY - 1:
                        split_w(2, 0)
                    if not first and n % GT < len(QUARTERS):
                        split_w(2 * i + 1 + n // GT, 1 - n // GT, QUARTERS[n % GT])
                    both = proj_ps[n % 2][:, :].rearrange("p (g h f) -> p g h f", g=G, h=2)
                    dve.wait_ge(s_square, u + 1)
                    if after_start(u - 3):
                        dve.wait_ge(s_scaled, u - 3)
                    dve.tensor_tensor(straight[:, n % 4].rearrange("p (g d) -> p g d", g=G),
                                      proj_ps[n % 2][:, :].rearrange("p (g d) -> p g d", g=G),
                                      table[:, 2 * w, t:t + 1, :].to_broadcast([P, G, D]), ALU.mult)
                    if after_start(u - 1):
                        dve.wait_ge(s_rot, u - 1)
                    swapped = crossed[:, n % 2].rearrange("p (g h f) -> p g h f", g=G, h=2)
                    for half in range(2):
                        last = dve.tensor_tensor(
                            swapped[:, :, half, :], both[:, :, 1 - half, :],
                            table[:, 2 * w + 1, t:t + 1, half * H:(half + 1) * H].to_broadcast([P, G, H]),
                            ALU.mult)
                    last.then_inc(s_cross, 1)
                    dve.tensor_reduce(sumsq[:, n % 4], square[:, n % 2].rearrange("p (g d) -> p g d", g=G),
                                      AX_X, ALU.add).then_inc(s_sumsq, 1)
                    if new is not None and new > 0:
                        low_part(new)

            for i in range(GROUP_ITERS):
                units(i, 1 if i == GROUP_ITERS - 1 else 0)
            with dve.Fori(GROUP_ITERS, ITERS - 1) as i:
                units(i, 0)
            units(ITERS - 1, 1)
            dve.wait_ge(s_proj, QK_UNITS)
            split_w(STREAM - 1, 1)

            for r in range(RING):
                dve.wait_ge(s_stored[r], 16 * QK_UNITS // RING)
            for c in range(2):
                dve.wait_ge(s_x1out[c], 16 * NT // 2)
            dve.memset(vt[SEQ:2 * SEQ, :, NCH - 1], 0.0)
            dve.memset(vt[2 * SEQ:P, :, NCH - 1], 0.0)
            dve.memset(probs[:, :, KEYS:], 0.0)
            dve.memset(mask[:, :, L:], 0.0)
            dve.drain()
            dve.memset(low[:, :], 0.0).then_inc(s_blank, 1)
            dve.drain()

            def write_mask(b, c):
                dve.tensor_scalar(mask[:, c, 0:L], key_no, lens_f[:, bass.ds(b, 1)], MASKED, ALU.is_ge,
                                  ALU.mult)
                dve.drain()

            def split_k(t, n):
                hk, c, r = n % HK, n // HK % 2, n % 4
                dve.wait_ge(s_khi, TP * t + n + 1)
                dve.tensor_tensor(k_lo[:, r].rearrange("d (a b) -> d a b", b=PSIZE),
                                  kt[:, c, :, hk * PSIZE:(hk + 1) * PSIZE],
                                  k_hi[:, r].bitcast(F32).rearrange("d (a b) -> d a b", b=PSIZE),
                                  ALU.subtract).then_inc(s_klo, 1)

            def split_q(t, m, h):
                c, cols = m % 2, slice(h * Q_COLS // 2, (h + 1) * Q_COLS // 2)
                dve.wait_ge(s_qhi, 2 * (TB * t + m) + h + 1)
                dve.tensor_tensor(q_lo[:, c, cols], q_raw[:, c, cols], q_hi[:, c, cols].bitcast(F32),
                                  ALU.subtract).then_inc(s_qlo, 1)

            def slot(t, n, do_pair, do_inverse, do_split, do_o):
                p = TP * t + n
                if do_inverse:
                    dve.wait_ge(s_exp, p)
                if do_pair:
                    dve.wait_ge(s_scores, p + 1)
                if do_inverse:
                    dve.reciprocal(inverse[:, (n - 1) % 4:(n - 1) % 4 + 1],
                                   total[:, (n - 1) % 4:(n - 1) % 4 + 1]).then_inc(s_inv, 1)
                if do_pair:
                    dve.tensor_tensor_reduce(probs[:, n % 4, 0:KEYS], scores_ps, mask[:, n // HK % 2],
                                             -SCALE, 3e38, ALU.add, ALU.min, low[:, n % 4:n % 4 + 1])\
                       .then_inc(s_low, 1)
                if do_split:
                    split_k(t, n + 2)
                if n % HK - 1 in Q_SPLITS and not last_sequence(t, n):
                    split_q(t, n // HK + 1, n % HK - 1 - Q_SPLITS[0])
                if n % HK == Q_SPLITS[1] + 2 and not last_sequence(t, n):
                    write_mask(TB * t + n // HK + 1, (n // HK + 1) % 2)
                if do_o:
                    k = (n - 3) % TP
                    b, hk = k // HK, k % HK
                    done = 2 * t + (n - 3) // (2 * HK)
                    dve.wait_ge(s_pv, p - 2)
                    if isinstance(p, int) and p == 3:
                        for c in range(2):
                            dve.wait_ge(s_vstored[c], 16 * (UNITS - QK_UNITS) // 2)
                    if hk == 0 and after_start(done):
                        dve.wait_ge(s_ostored[b % 2], 16 * done)
                    dve.tensor_copy(o_sb[:, b % 2, hk], o_ps[(n - 3) % 2][:, 0:P]).then_inc(s_o, 1)

            write_mask(0, 0)
            for h in range(2):
                split_q(0, 0, h)
            split_k(0, 0)
            split_k(0, 1)
            for n in range(TP):
                slot(0, n, True, n >= 1, True, n >= 3)
            with dve.Fori(1, NT - 1) as t:
                for n in range(TP):
                    slot(t, n, True, True, True, True)
            for n in range(TP + 3):
                slot(NT - 1, n, n < TP, n < TP + 1, n < TP - 2, True)

            def head(i, n):
                c, g, h = n // G, n % G, HEADS * i + n
                dve.wait_ge(s_ohi, h + 1)
                dve.tensor_tensor(o_lo[:, n % 2].rearrange("d (b s) -> d b s", s=SEQ),
                                  o_raw[c][:, :, g * SEQ:(g + 1) * SEQ],
                                  o_hi[:, n % 2].bitcast(F32).rearrange("d (b s) -> d b s", s=SEQ),
                                  ALU.subtract)
                dve.tensor_tensor(wo_lo[:, n % 2], wo_raw[c][:, g], wo_hi[:, n % 2].bitcast(F32),
                                  ALU.subtract).then_inc(s_olo, 1)

            for n in range(HEADS):
                head(0, n)
                if n == 1:
                    dve.memset(w2_sb[:, :], 0.0).then_inc(s_w2blank, 1)
            with dve.Fori(1, HK // 2) as i:
                for n in range(HEADS):
                    head(i, n)
            dve.wait_ge(s_late, 16 * 4)
            for t in range(NT):
                dve.wait_ge(s_acc, t + 1)
                dve.tensor_tensor(res2[:, t], acc[t][:, :], res1[:, t], ALU.add).then_inc(s_res2, 1)
            for t in range(NT):
                dve.wait_ge(s_l2, t + 1)
                dve.tensor_tensor(res3[:, t], acc[t][:, :], res2[:, t], ALU.add).then_inc(s_res3, 1)
            for t in range(NT):
                dve.wait_ge(s_hid, t + 1)
                dve.tensor_copy(hid[:, t], acc[t][:, 0:ER + E]).then_inc(s_hidc, 1)
            dve.drain()
            dve.tensor_tensor(logits[:, :, :], hid[:, :, ER:], lang_bias[:, :, :], ALU.add)
            dve.drain()
            for t in range(NT):
                dve.max(top[:, t], logits[:, t])
            dve.drain()
            dve.tensor_tensor(gate[:, 0], top[:, :, 1], top[:, :, 0], ALU.subtract).then_inc(s_gap, 1)
            for t in range(NT):
                dve.max_index(top_at[:, t], top[:, t], logits[:, t])
            dve.drain()
            dve.tensor_copy(top_f[:, :, :], top_at[:, :, :])
            dve.wait_ge(s_gexp, 1)
            dve.tensor_scalar(gate[:, 2], gate[:, 1], 1.0, None, ALU.add)
            dve.drain()
            dve.reciprocal(gate[:, 3], gate[:, 2])
            for x in range(2):
                dve.tensor_tensor(picks[:, x], expert_no.unsqueeze(1).to_broadcast([P, NT, E]),
                                  top_f[:, :, x:x + 1].to_broadcast([P, NT, E]), ALU.is_equal)
            dve.drain()
            dve.tensor_tensor(gate[:, 4], gate[:, 1], gate[:, 3], ALU.mult)
            dve.drain()
            for x in range(2):
                dve.tensor_tensor(picks[:, x], picks[:, x],
                                  gate[:, 3 + x].unsqueeze(2).to_broadcast([P, NT, E]), ALU.mult)
            dve.drain()
            dve.tensor_tensor(picks[:, 0], picks[:, 0], picks[:, 1], ALU.add)
            dve.drain()
            for t in range(NT):
                hidden = hid[:, t, 0:ER].rearrange("p (e r) -> p e r", e=E)
                last = dve.scalar_tensor_tensor(out=hidden, in0=hidden, scalar=SCALING,
                                                in1=picks[:, 0, t].unsqueeze(2).to_broadcast([P, E, R]),
                                                op0=ALU.mult, op1=ALU.mult)
            last.then_inc(s_gated, 1)
            dve.wait_ge(s_gturn, 1)
            for t in range(0, NT, 4):
                last = dve.tensor_copy(gated_t[:, t:t + 4],
                                       acc[NT - 2 + t // 4][:, :].rearrange("p (t n) -> p t n", n=P))
            last.then_inc(s_gt, 1)
            for t in range(NT):
                dve.wait_ge(s_l3, t + 1)
                dve.tensor_tensor(res1[:, t], acc[t][:, :], res3[:, t], ALU.add).then_inc(s_final, 1)


def kernel(**inputs):
    import concourse.bacc as bacc
    from concourse.bass_utils import run_bass_kernel_spmd

    def arr(name):
        return np.asarray(inputs[name])

    def feature_chunks(w):
        return w.T.reshape(KC, P, -1).transpose(1, 0, 2)

    x = arr("x").reshape(NB * SEQ, HID)
    w0 = arr("L0_cond_weight")
    qkv = np.concatenate([arr("L1_cond_Wq"), arr("L1_cond_Wk"), arr("L1_cond_Wv")])
    consts = np.zeros((P, C_ALL), np.float32)
    consts[:, C_IDENT:C_IDENT + P] = np.eye(P)
    power = (10000.0 ** (np.arange(0, D, 2) / D)).astype(np.float32)
    consts[:, C_FREQ:C_FREQ + D // 2] = np.float32(1.0) / power
    consts[:, C_KEY:C_KEY + L] = np.arange(L)
    consts[:, C_EXPERT:C_EXPERT + E] = np.arange(E)
    consts[:, C_TOKEN] = np.arange(P) % SEQ
    arrays = {
        "x_tok": x,
        "x_feat": feature_chunks(x),
        "adapter": arr("itok_B_0_15").reshape(1, NB),
        "pages": arr("itok_Bx16_0_63").reshape(1, NB * NPP),
        "lens": arr("itok_B_207_1644").reshape(1, NB),
        "subject": arr("itok_B_0_30").reshape(1, NB),
        "language": arr("itok_B_0_7").reshape(1, NB),
        "w0": w0.transpose(0, 2, 1).reshape(-1, KC, P, HID).transpose(0, 2, 1, 3),
        "wqkv": qkv.reshape(QKV_BLOCKS, HID, KC, P).transpose(0, 3, 2, 1).reshape(QKV_BLOCKS, P, KC * HID),
        "wo": arr("L1_cond_Wo").reshape(HID, HQ, D).transpose(2, 1, 0),
        "kcache": arr("L1_cond_k_cache").transpose(0, 3, 2, 1).reshape(PAGES, D, HK * PSIZE),
        "vcache": arr("L1_cond_v_cache").reshape(PAGES * PSIZE, HK * D),
        "q_w": arr("L1_cond_q_norm_w").reshape(1, D),
        "k_w": arr("L1_cond_k_norm_w").reshape(1, D),
        "w2": arr("L2_cond_weights"),
        "w3": feature_chunks(arr("L3_cond_W")),
        "a3": feature_chunks(np.concatenate([arr("L3_cond_A").reshape(ER, HID), arr("L3_cond_Wr")])),
        "b3": arr("L3_cond_B").transpose(0, 2, 1).reshape(ER, HID),
        "consts": consts,
    }
    arrays = {k: np.ascontiguousarray(v) for k, v in arrays.items()}
    nc = bacc.Bacc("TRN2", target_bir_lowering=False, num_devices=1)
    aps = {k: nc.dram_tensor(k, v.shape, mybir.dt.from_np(v.dtype), kind="ExternalInput").ap()
           for k, v in arrays.items()}
    out = nc.dram_tensor("out", (NB * SEQ, HID), F32, kind="ExternalOutput").ap()
    build(nc, out=out, **aps)
    got = run_bass_kernel_spmd(nc, [arrays], core_ids=[0]).results[0]["out"]
    return got.reshape(NB, SEQ, HID)
```
